# Optimizing a Trainium2 kernel written in Bass

```python
import numpy as np
import jax
import jax.numpy as jnp

def _softmax(x, axis=-1):
    return jax.nn.softmax(x, axis=axis)
def _gelu(x):
    return jax.nn.gelu(x, approximate=True)
def _silu(x):
    return jax.nn.silu(x)
def _sigmoid(x):
    return jax.nn.sigmoid(x)
def _layernorm(x, axis=-1, eps=1e-5):
    m = jnp.mean(x, axis=axis, keepdims=True)
    v = jnp.var(x, axis=axis, keepdims=True)
    return (x - m) / jnp.sqrt(v + eps)
def _scatter_add(tgt, idx, src, axis=0):
    return tgt.at[idx].add(src)
def _segment_sum(src, seg, n):
    return jax.ops.segment_sum(src, seg, n)

kernel_name = 'mk_conv_preact_d2_conv_nchw192_cf5e6d'

def setup_inputs(seed: int = 0):
    np.random.seed(seed)
    _w = jnp.asarray
    def _rec_inputs():
        import jax
        import jax.numpy as jnp
        _gk = jax.random.key(seed)
        x = 7.572e-06 + 1 * jax.random.normal(jax.random.fold_in(_gk, 1), (16, 192, 56, 56), jnp.float32)
        return x
    x = _rec_inputs()
    def _L0_conv_setup():
        import jax, jax.numpy as jnp
        import numpy as np
        LN_EPS = 1e-05
        NEG_INF = -1e+38

        def wkv_scan(w, u, k, v):
            Bdim, T, C = k.shape

            def step(carry, kv_t):
                p, q, o = carry
                kt, vt = kv_t
                no = jnp.maximum(o, u + kt)
                A = jnp.exp(o - no)
                Bw = jnp.exp(u + kt - no)
                y = (A * p + Bw * vt) / (A * q + Bw)
                no2 = jnp.maximum(w + o, kt)
                A2 = jnp.exp(w + o - no2)
                B2 = jnp.exp(kt - no2)
                return ((A2 * p + B2 * vt, A2 * q + B2, no2), y)
            init = (jnp.zeros((Bdim, C), k.dtype), jnp.zeros((Bdim, C), k.dtype), jnp.full((Bdim, C), NEG_INF, k.dtype))
            kT = jnp.moveaxis(k, 1, 0)
            vT = jnp.moveaxis(v, 1, 0)
            _, ys = jax.lax.scan(step, init, (kT, vT))
            return jnp.moveaxis(ys, 0, 1)
        key = jax.random.key(seed)
        ks = jax.random.split(key, 8)
        B, C, H, W = (16, 192, 56, 56)
        s = 0.02
        x = jax.random.normal(ks[0], (B, C, H, W), jnp.float32)
        Wk = jax.random.normal(ks[1], (C, C), jnp.float32) * s
        Wv = jax.random.normal(ks[2], (C, C), jnp.float32) * s
        Wr = jax.random.normal(ks[3], (C, C), jnp.float32) * s
        Wo = jax.random.normal(ks[4], (C, C), jnp.float32) * s
        ln_g = jnp.ones((C,), jnp.float32)
        ln_b = jnp.zeros((C,), jnp.float32)
        w_decay = -6.0 + 0.1 * jax.random.normal(ks[5], (C,), jnp.float32)
        u = 0.1 * jax.random.normal(ks[6], (C,), jnp.float32)
        return {'x': x, 'Wk': Wk, 'Wv': Wv, 'Wr': Wr, 'Wo': Wo, 'ln_g': ln_g, 'ln_b': ln_b, 'w_decay': w_decay, 'u': u}
    _L0_conv_all = _L0_conv_setup()
    _L0_conv_in = {k: v for k, v in _L0_conv_all.items() if k in ('Wk', 'Wv', 'Wr', 'Wo', 'ln_g', 'ln_b', 'w_decay', 'u', )}
    del _L0_conv_all

    def _L1_conv_setup():
        import jax, jax.numpy as jnp
        import numpy as np
        DIM = 192
        D_INNER = 2 * DIM
        D_STATE = 16
        D_CONV = 4
        DT_RANK = (DIM + 15) // 16
        B, H, W = (8, 64, 64)

        def _layernorm(x, g, b, eps=1e-05):
            mu = jnp.mean(x, -1, keepdims=True)
            var = jnp.mean(jnp.square(x - mu), -1, keepdims=True)
            return (x - mu) * jax.lax.rsqrt(var + eps) * g + b

        def _selective_scan(x, dt, Bc, Cc, A, D):
            b, L, d = x.shape
            n = A.shape[1]

            def step(h, inp):
                x_t, dt_t, B_t, C_t = inp
                dA = jnp.exp(dt_t[:, :, None] * A)
                h = h * dA + (dt_t * x_t)[:, :, None] * B_t[:, None, :]
                y = jnp.einsum('bdn,bn->bd', h, C_t)
                return (h, y)
            h0 = jnp.zeros((b, d, n), x.dtype)
            xs = (x.transpose(1, 0, 2), dt.transpose(1, 0, 2), Bc.transpose(1, 0, 2), Cc.transpose(1, 0, 2))
            _, ys = jax.lax.scan(step, h0, xs)
            return ys.transpose(1, 0, 2) + x * D

        def _branch(x, conv_w, conv_b, W_xproj, W_dt, dt_bias, A_log, D):
            L = x.shape[1]
            xp = jnp.pad(x, ((0, 0), (D_CONV - 1, 0), (0, 0)))
            xc = conv_b + sum((xp[:, k:k + L, :] * conv_w[:, k] for k in range(D_CONV)))
            xc = jax.nn.silu(xc)
            dbl = xc @ W_xproj.T
            dt = jax.nn.softplus(dbl[..., :DT_RANK] @ W_dt.T + dt_bias)
            Bc = dbl[..., DT_RANK:DT_RANK + D_STATE]
            Cc = dbl[..., DT_RANK + D_STATE:]
            A = -jnp.exp(A_log)
            return _selective_scan(xc, dt, Bc, Cc, A, D)
        key = jax.random.key(seed)
        ks = iter(jax.random.split(key, 32))

        def rn(shape, scale=0.02):
            return scale * jax.random.normal(next(ks), shape, dtype=jnp.float32)
        inp = {'x_embed_conv': jax.random.normal(next(ks), (B, DIM, H, W), dtype=jnp.float32), 'g1': jnp.ones((DIM,), jnp.float32), 'b1': jnp.zeros((DIM,), jnp.float32), 'g2': jnp.ones((DIM,), jnp.float32), 'b2': jnp.zeros((DIM,), jnp.float32), 'W_in_x': rn((D_INNER, DIM)), 'W_in_z': rn((D_INNER, DIM)), 'W_out': rn((DIM, D_INNER)), 'b_out': jnp.zeros((DIM,), jnp.float32)}
        A_init = jnp.log(jnp.tile(jnp.arange(1, D_STATE + 1, dtype=jnp.float32), (D_INNER, 1)))
        dt_bias_init = jnp.log(jnp.expm1(jnp.full((D_INNER,), 0.01, jnp.float32)))
        for sfx in ('f', 'b'):
            inp[f'conv_w_{sfx}'] = rn((D_INNER, D_CONV), 0.1)
            inp[f'conv_b_{sfx}'] = jnp.zeros((D_INNER,), jnp.float32)
            inp[f'W_xproj_{sfx}'] = rn((DT_RANK + 2 * D_STATE, D_INNER))
            inp[f'W_dt_{sfx}'] = rn((D_INNER, DT_RANK), 0.1)
            inp[f'dt_bias_{sfx}'] = dt_bias_init
            inp[f'A_log_{sfx}'] = A_init
            inp[f'D_{sfx}'] = jnp.ones((D_INNER,), jnp.float32)
        return inp
    _L1_conv_all = _L1_conv_setup()
    _L1_conv_in = {k: v for k, v in _L1_conv_all.items() if k in ('g1', 'b1', 'g2', 'b2', 'W_in_x', 'W_in_z', 'conv_w_f', 'conv_b_f', 'W_xproj_f', 'W_dt_f', 'dt_bias_f', 'A_log_f', 'D_f', 'conv_w_b', 'conv_b_b', 'W_xproj_b', 'W_dt_b', 'dt_bias_b', 'A_log_b', 'D_b', 'W_out', 'b_out', )}
    del _L1_conv_all

    return {
        "x": x,
        "L0_conv_Wk": _L0_conv_in["Wk"],
        "L0_conv_Wv": _L0_conv_in["Wv"],
        "L0_conv_Wr": _L0_conv_in["Wr"],
        "L0_conv_Wo": _L0_conv_in["Wo"],
        "L0_conv_ln_g": _L0_conv_in["ln_g"],
        "L0_conv_ln_b": _L0_conv_in["ln_b"],
        "L0_conv_w_decay": _L0_conv_in["w_decay"],
        "L0_conv_u": _L0_conv_in["u"],
        "L1_conv_g1": _L1_conv_in["g1"],
        "L1_conv_b1": _L1_conv_in["b1"],
        "L1_conv_g2": _L1_conv_in["g2"],
        "L1_conv_b2": _L1_conv_in["b2"],
        "L1_conv_W_in_x": _L1_conv_in["W_in_x"],
        "L1_conv_W_in_z": _L1_conv_in["W_in_z"],
        "L1_conv_conv_w_f": _L1_conv_in["conv_w_f"],
        "L1_conv_conv_b_f": _L1_conv_in["conv_b_f"],
        "L1_conv_W_xproj_f": _L1_conv_in["W_xproj_f"],
        "L1_conv_W_dt_f": _L1_conv_in["W_dt_f"],
        "L1_conv_dt_bias_f": _L1_conv_in["dt_bias_f"],
        "L1_conv_A_log_f": _L1_conv_in["A_log_f"],
        "L1_conv_D_f": _L1_conv_in["D_f"],
        "L1_conv_conv_w_b": _L1_conv_in["conv_w_b"],
        "L1_conv_conv_b_b": _L1_conv_in["conv_b_b"],
        "L1_conv_W_xproj_b": _L1_conv_in["W_xproj_b"],
        "L1_conv_W_dt_b": _L1_conv_in["W_dt_b"],
        "L1_conv_dt_bias_b": _L1_conv_in["dt_bias_b"],
        "L1_conv_A_log_b": _L1_conv_in["A_log_b"],
        "L1_conv_D_b": _L1_conv_in["D_b"],
        "L1_conv_W_out": _L1_conv_in["W_out"],
        "L1_conv_b_out": _L1_conv_in["b_out"],
    }

def reference(x, L0_conv_Wk, L0_conv_Wv, L0_conv_Wr, L0_conv_Wo, L0_conv_ln_g, L0_conv_ln_b, L0_conv_w_decay, L0_conv_u, L1_conv_g1, L1_conv_b1, L1_conv_g2, L1_conv_b2, L1_conv_W_in_x, L1_conv_W_in_z, L1_conv_conv_w_f, L1_conv_conv_b_f, L1_conv_W_xproj_f, L1_conv_W_dt_f, L1_conv_dt_bias_f, L1_conv_A_log_f, L1_conv_D_f, L1_conv_conv_w_b, L1_conv_conv_b_b, L1_conv_W_xproj_b, L1_conv_W_dt_b, L1_conv_dt_bias_b, L1_conv_A_log_b, L1_conv_D_b, L1_conv_W_out, L1_conv_b_out):
    import jax
    import jax.numpy as jnp
    def _L0_conv_ref(x, Wk, Wv, Wr, Wo, ln_g, ln_b, w_decay, u):
        import jax, jax.numpy as jnp
        import numpy as np
        LN_EPS = 1e-05
        NEG_INF = -1e+38

        def wkv_scan(w, u, k, v):
            Bdim, T, C = k.shape

            def step(carry, kv_t):
                p, q, o = carry
                kt, vt = kv_t
                no = jnp.maximum(o, u + kt)
                A = jnp.exp(o - no)
                Bw = jnp.exp(u + kt - no)
                y = (A * p + Bw * vt) / (A * q + Bw)
                no2 = jnp.maximum(w + o, kt)
                A2 = jnp.exp(w + o - no2)
                B2 = jnp.exp(kt - no2)
                return ((A2 * p + B2 * vt, A2 * q + B2, no2), y)
            init = (jnp.zeros((Bdim, C), k.dtype), jnp.zeros((Bdim, C), k.dtype), jnp.full((Bdim, C), NEG_INF, k.dtype))
            kT = jnp.moveaxis(k, 1, 0)
            vT = jnp.moveaxis(v, 1, 0)
            _, ys = jax.lax.scan(step, init, (kT, vT))
            return jnp.moveaxis(ys, 0, 1)
        B, C, H, W = x.shape
        xs = jnp.transpose(x.reshape(B, C, H * W), (0, 2, 1))
        k = jnp.einsum('btc,dc->btd', xs, Wk)
        v = jnp.einsum('btc,dc->btd', xs, Wv)
        r = jnp.einsum('btc,dc->btd', xs, Wr)
        real_w = -jnp.exp(w_decay)
        x_fwd = wkv_scan(real_w, u, k, v)
        x_bwd = jnp.flip(wkv_scan(real_w, u, jnp.flip(k, 1), jnp.flip(v, 1)), 1)
        x_bi = 0.5 * (x_fwd + x_bwd)
        h = jax.nn.sigmoid(r) * x_bi
        mu = jnp.mean(h, axis=-1, keepdims=True)
        var = jnp.var(h, axis=-1, keepdims=True)
        h = (h - mu) * jax.lax.rsqrt(var + LN_EPS) * ln_g + ln_b
        out = jnp.einsum('btc,dc->btd', h, Wo)
        return jnp.transpose(out, (0, 2, 1)).reshape(B, C, H, W)

    def _L1_conv_ref(x_embed_conv, g1, b1, g2, b2, W_in_x, W_in_z, conv_w_f, conv_b_f, W_xproj_f, W_dt_f, dt_bias_f, A_log_f, D_f, conv_w_b, conv_b_b, W_xproj_b, W_dt_b, dt_bias_b, A_log_b, D_b, W_out, b_out):
        import jax, jax.numpy as jnp
        import numpy as np
        DIM = 192
        D_INNER = 2 * DIM
        D_STATE = 16
        D_CONV = 4
        DT_RANK = (DIM + 15) // 16
        B, H, W = (8, 64, 64)

        def _layernorm(x, g, b, eps=1e-05):
            mu = jnp.mean(x, -1, keepdims=True)
            var = jnp.mean(jnp.square(x - mu), -1, keepdims=True)
            return (x - mu) * jax.lax.rsqrt(var + eps) * g + b

        def _selective_scan(x, dt, Bc, Cc, A, D):
            b, L, d = x.shape
            n = A.shape[1]

            def step(h, inp):
                x_t, dt_t, B_t, C_t = inp
                dA = jnp.exp(dt_t[:, :, None] * A)
                h = h * dA + (dt_t * x_t)[:, :, None] * B_t[:, None, :]
                y = jnp.einsum('bdn,bn->bd', h, C_t)
                return (h, y)
            h0 = jnp.zeros((b, d, n), x.dtype)
            xs = (x.transpose(1, 0, 2), dt.transpose(1, 0, 2), Bc.transpose(1, 0, 2), Cc.transpose(1, 0, 2))
            _, ys = jax.lax.scan(step, h0, xs)
            return ys.transpose(1, 0, 2) + x * D

        def _branch(x, conv_w, conv_b, W_xproj, W_dt, dt_bias, A_log, D):
            L = x.shape[1]
            xp = jnp.pad(x, ((0, 0), (D_CONV - 1, 0), (0, 0)))
            xc = conv_b + sum((xp[:, k:k + L, :] * conv_w[:, k] for k in range(D_CONV)))
            xc = jax.nn.silu(xc)
            dbl = xc @ W_xproj.T
            dt = jax.nn.softplus(dbl[..., :DT_RANK] @ W_dt.T + dt_bias)
            Bc = dbl[..., DT_RANK:DT_RANK + D_STATE]
            Cc = dbl[..., DT_RANK + D_STATE:]
            A = -jnp.exp(A_log)
            return _selective_scan(xc, dt, Bc, Cc, A, D)
        b, c, h, w = x_embed_conv.shape
        tok = x_embed_conv.reshape(b, c, h * w).transpose(0, 2, 1)
        x1 = _layernorm(tok, g1, b1)
        x2 = _layernorm(tok, g2, b2)
        x = x1 @ W_in_x.T
        z = x2 @ W_in_z.T
        y_f = _branch(x, conv_w_f, conv_b_f, W_xproj_f, W_dt_f, dt_bias_f, A_log_f, D_f)
        y_b = _branch(x[:, ::-1, :], conv_w_b, conv_b_b, W_xproj_b, W_dt_b, dt_bias_b, A_log_b, D_b)[:, ::-1, :]
        y = (y_f + y_b) * jax.nn.silu(z)
        out = y @ W_out.T + b_out
        return out.transpose(0, 2, 1).reshape(b, c, h, w)

    def _gn(v, G=32, eps=1e-5):
        B_, C_, H_, W_ = v.shape
        g = v.reshape(B_, G, C_ // G, H_, W_)
        m = jnp.mean(g, axis=(2, 3, 4), keepdims=True)
        s = jnp.var(g, axis=(2, 3, 4), keepdims=True)
        return ((g - m) / jnp.sqrt(s + eps)).reshape(v.shape)

    def _ln_c(v, eps=1e-6):
        m = jnp.mean(v, axis=1, keepdims=True)
        s = jnp.var(v, axis=1, keepdims=True)
        return (v - m) / jnp.sqrt(s + eps)

    def _ln_t(v, eps=1e-5):
        m = jnp.mean(v, axis=-1, keepdims=True)
        s = jnp.var(v, axis=-1, keepdims=True)
        return (v - m) / jnp.sqrt(s + eps)

    def _to_tokens(v):
        B_, C_, H_, W_ = v.shape
        return v.reshape(B_, C_, H_ * W_).transpose(0, 2, 1)
    def _from_tokens(t, like):
        B_, C_, H_, W_ = like.shape
        return t.transpose(0, 2, 1).reshape(B_, C_, H_, W_)

    x = x + _L0_conv_ref(_gn(x), L0_conv_Wk, L0_conv_Wv, L0_conv_Wr, L0_conv_Wo, L0_conv_ln_g, L0_conv_ln_b, L0_conv_w_decay, L0_conv_u)
    x = x + _L1_conv_ref(_gn(x), L1_conv_g1, L1_conv_b1, L1_conv_g2, L1_conv_b2, L1_conv_W_in_x, L1_conv_W_in_z, L1_conv_conv_w_f, L1_conv_conv_b_f, L1_conv_W_xproj_f, L1_conv_W_dt_f, L1_conv_dt_bias_f, L1_conv_A_log_f, L1_conv_D_f, L1_conv_conv_w_b, L1_conv_conv_b_b, L1_conv_W_xproj_b, L1_conv_W_dt_b, L1_conv_dt_bias_b, L1_conv_A_log_b, L1_conv_D_b, L1_conv_W_out, L1_conv_b_out)
    return x


_drawn_inputs = setup_inputs


def setup_inputs(seed=0):
    import zlib

    import numpy as np

    out = dict(_drawn_inputs(seed))
    spreads = {'L0_conv_ln_g': (1.0, 0.2),
     'L0_conv_ln_b': (0.0, 0.1),
     'L1_conv_g1': (1.0, 0.2),
     'L1_conv_b1': (0.0, 0.1),
     'L1_conv_g2': (1.0, 0.2),
     'L1_conv_b2': (0.0, 0.1),
     'L1_conv_conv_b_f': (0.0, 0.1),
     'L1_conv_dt_bias_f': (-4.600166320800781, 0.2),
     'L1_conv_D_f': (1.0, 0.2),
     'L1_conv_conv_b_b': (0.0, 0.1),
     'L1_conv_dt_bias_b': (-4.600166320800781, 0.2),
     'L1_conv_D_b': (1.0, 0.2),
     'L1_conv_b_out': (0.0, 0.1)}
    factors = {}
    for name, (base, spread) in spreads.items():
        noise = np.random.default_rng([zlib.crc32(name.encode()), seed]).standard_normal(out[name].shape)
        drawn = base * np.exp(spread * noise) if base else spread * noise
        out[name] = jnp.asarray(drawn.astype(out[name].dtype))
    for name, factor in factors.items():
        out[name] = (out[name] * factor).astype(out[name].dtype)
    return out
```

```python
from contextlib import ExitStack

import concourse.bass as bass
from concourse import mybir

F32 = mybir.dt.float32
BF16 = mybir.dt.bfloat16
ALU = mybir.AluOpType
ACT = mybir.ActivationFunctionType

B, C, L = 16, 192, 3136
CP, CJ = 96, 2
T, NC = 448, 7
EJ = 3
NS = 16
R = 12
CLAMP = 30.0


class Mark:

    def __init__(self, sem, value):
        self.sem, self.value = sem, value


class Queue:

    def __init__(self, sem):
        self.sem, self.count, self.ops = sem, 0, []

    def do(self, fn, *waits, inc=True):
        if inc:
            self.count += 1
        self.ops.append((fn, waits, inc))
        return Mark(self.sem, self.count)

    def emit(self, eng):
        seen = {}
        for fn, waits, inc in self.ops:
            for m in waits:
                if seen.get(m.sem.num, 0) < m.value:
                    eng.wait_ge(m.sem, m.value)
                    seen[m.sem.num] = m.value
            ins = fn(eng)
            if inc:
                ins.then_inc(self.sem, 1)


def tt(q, out, a, b, op, *w):
    return q.do(lambda e: e.tensor_tensor(out, a, b, op), *w)


def stt(q, out, a, s, b, op0, op1, *w):
    return q.do(lambda e: e.scalar_tensor_tensor(out, a, s, b, op0, op1), *w)


def ts(q, out, a, s1, s2, op0, op1, *w):
    return q.do(lambda e: e.tensor_scalar(out, a, s1, s2, op0, op1), *w)


def scan(q, out, a, b, init, op0, op1, *w):
    return q.do(lambda e: e.tensor_tensor_scan(out, a, b, init, op0, op1), *w)


def copy(q, out, a, *w):
    return q.do(lambda e: e.tensor_copy(out, a), *w)


def fill(q, out, v, *w):
    return q.do(lambda e: e.memset(out, v), *w)


def act(q, out, a, f, *w, bias=0.0, scale=1.0):
    return q.do(lambda e: e.activation(out, a, f, bias=bias, scale=scale), *w)


def mm(q, out, lhsT, rhs, start, stop, *w, inc=None):
    return q.do(lambda e: e.matmul(out, lhsT, rhs, start=start, stop=stop), *w,
                inc=stop if inc is None else inc)


def rev(ap, backward):
    return ap[:, ::-1] if backward else ap


def program(nc, d):
    with ExitStack() as ctx:
        build(nc, d, ctx)


def build(nc, d, ctx):
    def sb(name, shape, dt=F32):
        return ctx.enter_context(nc.sbuf_tensor(name, shape, dt))

    def sem(name):
        return ctx.enter_context(nc.semaphore(name))

    ident = sb("ident", [128, 128])
    grp = sb("grp", [CP, CP])
    ones = sb("ones", [CP, CP])
    sel = sb("sel", [128, 2 * NS, 128], BF16)
    w0 = {m: sb("w0" + m, [CP, CJ, C]) for m in "kvro"}
    vec0 = sb("vec0", [CP, 8, CJ])
    wx = sb("wx", [CP, CJ, 384])
    wz = sb("wz", [CP, CJ, 384])
    vec1 = sb("vec1", [CP, 4, CJ])
    wout = sb("wout", [128, EJ, C])
    bxz = sb("bxz", [128, 3, EJ])
    xpw = [sb(f"xpw{s}", [128, EJ, 128]) for s in range(2)]
    wdt = [sb(f"wdt{s}", [R, 384]) for s in range(2)]
    Am = [sb(f"A{s}", [128, EJ, NS]) for s in range(2)]
    diag = [sb(f"diag{s}", [128, EJ, 4, 128]) for s in range(2)]
    vece = [sb(f"vece{s}", [128, 4, EJ]) for s in range(2)]
    mv = sb("mv", [CP, CJ, 2])
    gs = sb("gs", [CP, 6, CJ])
    st = sb("st", [CP, CJ, NC, 6])

    x1 = sb("x1", [CP, CJ, L])
    arena_n = 36032
    arena = sb("arena", [128, arena_n])
    ps = ctx.enter_context(nc.psum_tensor("ps", [128, 8, 512], F32))

    at = [0]

    def take(*shape, parts=128):
        n = 1
        for s in shape:
            n *= s
        o = at[0]
        at[0] += n
        assert at[0] <= arena_n, at[0]
        v = arena[0:parts, o:o + n]
        if len(shape) == 2:
            v = v.rearrange("p (a b) -> p a b", a=shape[0])
        elif len(shape) == 3:
            v = v.rearrange("p (a b c) -> p a b c", a=shape[0], b=shape[1])
        return v

    sems = {}
    for ph in "abc":
        for e in "vaptd":
            sems[ph + e] = sem(f"s_{ph}{e}")
    s_ld = [sem(f"s_ld{i}") for i in range(NC)]

    def queues(ph):
        return {e: Queue(sems[ph + e]) for e in "vapt"}

    q = queues("a")
    V, A, P, PE = q["v"], q["a"], q["p"], q["t"]
    loads = [
        (ident, d["c_ident"]), (grp, d["c_grp"]), (ones, d["c_ones"]), (sel, d["c_sel"]),
        (w0["k"], d["wk"]), (w0["v"], d["wv"]), (w0["r"], d["wr"]), (w0["o"], d["wo"]),
        (vec0[:, 0:4, :], d["vec0"]), (vec0[:, 7:8, :], d["b_out"]),
        (wx, d["wx"]), (wz, d["wz"]), (vec1, d["vec1"]), (wout, d["wout"]),
    ]
    for s in range(2):
        loads += [(xpw[s], d[f"xpw{s}"]), (wdt[s], d[f"wdt{s}"]), (Am[s], d[f"alog{s}"]),
                  (vece[s][:, 0:3, :], d[f"vece{s}"])]
    tap = take(2, EJ * 4)
    loads += [(tap[:, s, :], d[f"tap{s}"]) for s in range(2)]
    ld = Mark(sems["ad"], 16 * len(loads))

    m = act(A, vec0[:, 4, :], vec0[:, 2, :], ACT.Exp, ld)
    m = ts(V, vec0[:, 4, :], vec0[:, 4, :], -1.0, None, ALU.mult, ALU.bypass, m)
    m = tt(V, vec0[:, 5, :], vec0[:, 4, :], vec0[:, 3, :], ALU.add, ld, m)
    m = ts(V, vec0[:, 5, :], vec0[:, 5, :], 40.0, None, ALU.min, ALU.bypass, m)
    m = act(A, vec0[:, 5, :], vec0[:, 5, :], ACT.Exp, m)
    ts(V, vec0[:, 5, :], vec0[:, 5, :], -1.0, None, ALU.add, ALU.bypass, m)
    for o in range(CJ):
        for j in range(CJ):
            m_bo = mm(PE, ps[0:CP, 0, o:o + 1], w0["o"][:, j, o * CP:(o + 1) * CP],
                      vec0[:, 1, j:j + 1], j == 0, j == 1, ld)
    for i, (w, b) in enumerate(((wx, 1), (wz, 3))):
        for o in range(EJ):
            for j in range(CJ):
                m_bx = mm(PE, ps[:, 1 + i, o:o + 1], w[:, j, o * 128:(o + 1) * 128],
                          vec1[:, b, j:j + 1], j == 0, j == 1)
    copy(V, vec0[:, 6, :], ps[0:CP, 0, 0:CJ], m_bo)
    copy(V, bxz[:, 0, :], ps[:, 1, 0:EJ], m_bx)
    copy(V, bxz[:, 1, :], ps[:, 2, 0:EJ], m_bx)
    ts(V, bxz[:, 2, :], ps[:, 2, 0:EJ], CLAMP, None, ALU.add, ALU.bypass)
    for j in range(CJ):
        ts(V, w0["o"][:, j, :], w0["o"][:, j, :], vec0[:, 0, j:j + 1], None, ALU.mult, ALU.bypass, m_bo)
        ts(V, wx[:, j, :], wx[:, j, :], vec1[:, 0, j:j + 1], None, ALU.mult, ALU.bypass, m_bx)
        ts(V, wz[:, j, :], wz[:, j, :], vec1[:, 2, j:j + 1], None, ALU.mult, ALU.bypass, m_bx)
    for s in range(2):
        m = act(A, Am[s][:, :, :], Am[s][:, :, :], ACT.Exp, ld)
        ts(V, Am[s][:, :, :], Am[s][:, :, :], -1.0, None, ALU.mult, ALU.bypass, m)
        ts(V, vece[s][:, 3, :], vece[s][:, 0, :], CLAMP, None, ALU.add, ALU.bypass)
        for j in range(EJ):
            for k in range(4):
                ts(V, diag[s][:, j, k, :], ident[:, :], tap[:, s, 4 * j + k:4 * j + k + 1], None,
                   ALU.mult, ALU.bypass, ld)
    m_setup = [Mark(V.sem, V.count), Mark(A.sem, A.count)]

    with nc.Block() as blk:
        @blk.sync
        def _(e):
            for dst, src in loads:
                e.dma_start(dst[:], src).then_inc(sems["ad"], 16)
            for m in m_setup:
                e.wait_ge(m.sem, m.value)

        @blk.scalar
        def _(e):
            A.emit(e)

        @blk.vector
        def _(e):
            V.emit(e)

        @blk.tensor
        def _(e):
            PE.emit(e)

    def group_stats(V, A, PE, banks, after):
        dv, dv2, var = gs[:, 0, :], gs[:, 1, :], gs[:, 2, :]
        pm, pv = (ps[0:CP, b, 0:CJ] for b in banks)
        m1 = mm(PE, pm, grp[:, :], mv[:, :, 0], True, True, *after)
        m = tt(V, dv, mv[:, :, 0], pm, ALU.subtract, m1)
        m = tt(V, dv2, dv, dv, ALU.mult, m)
        m = tt(V, var, mv[:, :, 1], dv2, ALU.add, m)
        m = mm(PE, pv, grp[:, :], var, True, True, m)
        m = ts(V, gs[:, 3, :], pv, 1e-5, None, ALU.add, ALU.bypass, m)
        m = act(A, gs[:, 3, :], gs[:, 3, :], ACT.Ln, m)
        m = act(A, gs[:, 4, :], gs[:, 3, :], ACT.Exp, m, scale=-0.5)
        return stt(V, gs[:, 5, :], pm, -1.0, gs[:, 4, :], ALU.mult, ALU.mult, m)

    def ch(c):
        return slice(c * T, (c + 1) * T)

    def layer0():
        at[0] = 0
        q = queues("b")
        V, A, P, PE = q["v"], q["a"], q["p"], q["t"]
        xn = take(CJ, L, parts=CP)
        kk = take(CJ, L, parts=CP)
        vv = take(CJ, L, parts=CP)
        sg = take(CJ, L, parts=CP)
        Oc = take(3, T + 1, parts=CP)
        s1 = take(3, T, parts=CP)
        s2 = take(3, T, parts=CP)
        bv = take(3, T, parts=CP)
        pp = take(3, T, parts=CP)
        qq = take(3, T, parts=CP)
        lt = take(T, parts=CP)
        tn = take(2, T, parts=CP)

        for c in range(NC):
            for j in range(CJ):
                m = V.do(lambda e, c=c, j=j: e.bn_stats(st[:, j, c, :], x1[:, j, ch(c)]), Mark(s_ld[c], 16))
        for j in range(CJ):
            m2 = V.do(lambda e, j=j: e.bn_aggr(mv[:, j, :], st[:, j, :, :].rearrange("p a b -> p (a b)")), m)
        m_g = group_stats(V, A, PE, (0, 1), [m2])
        m_xn = {}
        for c in range(NC):
            for j in range(CJ):
                m_xn[c] = ts(V, xn[:, j, ch(c)], x1[:, j, ch(c)], gs[:, 4, j:j + 1], gs[:, 5, j:j + 1],
                             ALU.mult, ALU.add, m_g)

        bank_free = [None] * 8
        nb = [0]

        def bank():
            i = 2 + nb[0] % 6
            nb[0] += 1
            return i, [bank_free[i]] if bank_free[i] else []

        m_kv = {}

        def project(c):
            for j in range(CJ):
                for name, dst in (("k", kk), ("v", vv), ("r", sg)):
                    b, free = bank()
                    out = ps[0:CP, b, 0:T]
                    for i in range(CJ):
                        m = mm(PE, out, w0[name][:, i, j * CP:(j + 1) * CP], xn[:, i, ch(c)],
                               i == 0, i == 1, m_xn[c], *free)
                    o = dst[:, j, ch(c)]
                    if name == "r":
                        m = act(A, o, out, ACT.Relu, m, bias=CLAMP)
                        bank_free[b] = m
                        m = act(A, o, o, ACT.Exp, m, scale=-1.0, bias=CLAMP)
                        m = act(A, o, o, ACT.Ln, m, bias=1.0)
                        m_kv[name, c, j] = act(A, o, o, ACT.Exp, m, scale=-1.0)
                    else:
                        m_kv[name, c, j] = bank_free[b] = act(A, o, out, ACT.Copy, m)

        units = [(0, c, j) for c in range(NC) for j in range(CJ)]
        units += [(1, c, j) for c in reversed(range(NC)) for j in range(CJ)]
        mO, ms, mB, mP, mN, mD, mR, mT, mY = ({} for _ in range(9))

        def stage1(u):
            s, c, j = units[u]
            r = u % 3
            first = c == (NC - 1 if s else 0)
            edge = T if s else 0
            cur = Oc[:, r, 0:T] if s else Oc[:, r, 1:T + 1]
            prv = Oc[:, r, 1:T + 1] if s else Oc[:, r, 0:T]
            free = [ms[u - 3]] if u >= 3 else []
            if first:
                m = fill(V, Oc[:, r, edge:edge + 1], -1e38, *free)
                init = -1e38
            else:
                ro = (u - 2) % 3
                last = 0 if s else T
                m = copy(V, Oc[:, r, edge:edge + 1], Oc[:, ro, last:last + 1], mO[u - 2], *free)
                init = Oc[:, ro, last:last + 1]
            mO[u] = scan(V, rev(cur, s), vec0[:, 4, j:j + 1].to_broadcast([CP, T]), rev(kk[:, j, ch(c)], s),
                         init, ALU.add, ALU.max, m_kv["k", c, j], m)
            free = [mT[u - 3], mD[u - 3]] if u >= 3 else []
            m1 = tt(P, s1[:, r, :], prv, cur, ALU.subtract, mO[u], *free)
            m2 = ms[u] = tt(P, s2[:, r, :], kk[:, j, ch(c)], cur, ALU.subtract)
            act(A, s1[:, r, :], s1[:, r, :], ACT.Exp, m1, bias=vec0[:, 4, j:j + 1])
            mB[u] = act(A, s2[:, r, :], s2[:, r, :], ACT.Exp, m2)

        def stage2(u):
            s, c, j = units[u]
            r = u % 3
            first = c == (NC - 1 if s else 0)
            ro, last = (u - 2) % 3, 0 if s else T - 1
            free = [mY[u - 3]] if u >= 3 else []
            m = tt(V, bv[:, r, :], s2[:, r, :], vv[:, j, ch(c)], ALU.mult, mB[u], m_kv["v", c, j], *free)
            prev = [mP[u - 2]] if not first else []
            i0 = 0.0 if first else pp[:, ro, last:last + 1]
            i1 = 0.0 if first else qq[:, ro, last:last + 1]
            m0 = scan(V, rev(pp[:, r, :], s), rev(s1[:, r, :], s), rev(bv[:, r, :], s), i0,
                      ALU.mult, ALU.add, m, *prev)
            m1 = mP[u] = scan(V, rev(qq[:, r, :], s), rev(s1[:, r, :], s), rev(s2[:, r, :], s), i1,
                              ALU.mult, ALU.add)
            mN[u] = stt(V, bv[:, r, :], bv[:, r, :], vec0[:, 5, j:j + 1], pp[:, r, :], ALU.mult, ALU.add, m0)
            m = stt(V, s2[:, r, :], s2[:, r, :], vec0[:, 5, j:j + 1], qq[:, r, :], ALU.mult, ALU.add, m1)
            m = act(A, lt, s2[:, r, :], ACT.Ln, m, *([mR[u - 1]] if u else []))
            m = mR[u] = act(A, s1[:, r, :], lt, ACT.Exp, m, scale=-1.0)
            mD[u] = tt(P, tn[:, u % 2, :], s2[:, r, :], s1[:, r, :], ALU.mult, m,
                       *([mY[u - 2]] if u >= 2 else []))

        m_add = {}

        def stage3(u):
            s, c, j = units[u]
            r = u % 3
            t = tn[:, u % 2, :]
            m = mT[u] = stt(V, t, t, 2.0, s1[:, r, :], ALU.subtract, ALU.mult, mD[u])
            ya = xn[:, j, ch(c)]
            if not s:
                mY[u] = m_add[c, j] = tt(V, ya, bv[:, r, :], t, ALU.mult, m, mN[u], m_kv["r", c, CJ - 1])
            else:
                m = tt(V, t, bv[:, r, :], t, ALU.mult, m, mN[u])
                mY[u] = m_add[c, j] = tt(P, ya, ya, t, ALU.add, m, m_add[c, j])

        def finish(c):
            m = None
            for j in range(CJ):
                h = xn[:, j, ch(c)]
                m = stt(V, h, h, -0.5, sg[:, j, ch(c)], ALU.mult, ALU.mult, m_add[c, j], m_kv["r", c, j])
            b, free = bank()
            mean = ps[0:CP, b, 0:T]
            for j in range(CJ):
                m1 = mm(PE, mean, ones[:, :], xn[:, j, ch(c)], j == 0, j == 1, m, *free)
            for j in range(CJ):
                h = xn[:, j, ch(c)]
                m = tt(V, h, h, mean, ALU.subtract, m1)
                m2 = act(A, sg[:, j, ch(c)], h, ACT.Square, m)
            bank_free[b] = m_hc = m
            b, free = bank()
            var = ps[0:CP, b, 0:T]
            for j in range(CJ):
                m = mm(PE, var, ones[:, :], sg[:, j, ch(c)], j == 0, j == 1, m2, *free)
            rs = kk[:, 0, ch(c)]
            m = ts(V, rs, var, 1e-5, None, ALU.add, ALU.bypass, m)
            bank_free[b] = m
            m = act(A, rs, rs, ACT.Ln, m)
            m = act(A, rs, rs, ACT.Exp, m, scale=-0.5)
            for j in range(CJ):
                h = xn[:, j, ch(c)]
                m1 = tt(P, h, h, rs, ALU.mult, m, m_hc)
            for o in range(CJ):
                b, free = bank()
                out = ps[0:CP, b, 0:T]
                for j in range(CJ):
                    m = mm(PE, out, w0["o"][:, j, o * CP:(o + 1) * CP], xn[:, j, ch(c)],
                           j == 0, j == 1, m1, *free)
                x = x1[:, o, ch(c)]
                m = bank_free[b] = stt(V, x, out, vec0[:, 6, o:o + 1], x, ALU.add, ALU.add, m)
                V.do(lambda e, c=c, o=o: e.bn_stats(st[:, o, c, :], x1[:, o, ch(c)]), m)

        n = len(units)
        project(0)
        for u in range(n + 3):
            if u < n:
                if u % 2 == 0 and u // 2 + 1 < NC:
                    project(u // 2 + 1)
                stage1(u)
            if 1 <= u <= n:
                stage2(u - 1)
            if 2 <= u <= n + 1:
                stage3(u - 2)
            if u >= n // 2 + 4 and (u - n // 2) % 2 == 0:
                finish(units[u - 4][1])
        m = Mark(V.sem, V.count)
        for j in range(CJ):
            V.do(lambda e, j=j: e.bn_aggr(mv[:, j, :], st[:, j, :, :].rearrange("p a b -> p (a b)")), m)
        return q

    def layer1():
        at[0] = 0
        q = queues("c")
        V, A, P, PE = q["v"], q["a"], q["p"], q["t"]
        nrm = take(CJ, L, parts=CP)
        yf = take(EJ, L)
        xh = take(EJ, T + 3)
        xc = [take(EJ, T) for _ in range(2)]
        dt = [take(EJ, T) for _ in range(2)]
        du = [take(EJ, T) for _ in range(2)]
        bcp = [take(T // 2).bitcast(BF16) for _ in range(2)]
        mid = take(T // 2).bitcast(BF16)
        res = take(T)
        NCR, NDB, NH, NPR = 3, 5, 6, 3
        cr = take(NCR, T)
        bs = take(2, T)
        db = take(NDB, T)
        hh = take(NH, T)
        pr = take(NPR, T)
        g1 = take(T)
        g2 = take(T)
        car = take(NS, EJ)
        ybank, abank, bbank, wbank = (0, 1, 2), (3, 4), (5, 6), 7

        w_free = [None]

        def wb():
            return [w_free[0]] if w_free[0] else []

        pw = ps[:, wbank, :]
        m_g = group_stats(V, A, PE, (5, 6), [])
        m_nrm, m_xc, m_dt, m_du, m_bcp, m_halo = {}, {}, {}, {}, {}, {}
        last_exp, last_mb, m_back, m_y1 = {}, {}, {}, {}
        chunks = [(0, c) for c in range(NC)] + [(1, c) for c in reversed(range(NC))]

        def norm(c):
            for j in range(CJ):
                m = ts(V, nrm[:, j, ch(c)], x1[:, j, ch(c)], gs[:, 4, j:j + 1], gs[:, 5, j:j + 1],
                       ALU.mult, ALU.add, m_g)
            for j in range(CJ):
                m1 = mm(PE, pw[0:CP, 0:T], ones[:, :], nrm[:, j, ch(c)], j == 0, j == 1, m, *wb())
            for j in range(CJ):
                o = nrm[:, j, ch(c)]
                m = m_hc = w_free[0] = tt(V, o, o, pw[0:CP, 0:T], ALU.subtract, m1)
                sq = act(A, yf[0:CP, j, ch(c)], o, ACT.Square, m)
            yield
            for j in range(CJ):
                m = mm(PE, pw[0:CP, 0:T], ones[:, :], yf[0:CP, j, ch(c)], j == 0, j == 1, sq, *wb())
            rs = yf[0:CP, 2, ch(c)]
            m = w_free[0] = ts(V, rs, pw[0:CP, 0:T], 1e-5, None, ALU.add, ALU.bypass, m)
            m = act(A, rs, rs, ACT.Ln, m)
            m = act(A, rs, rs, ACT.Exp, m, scale=-0.5)
            for j in range(CJ):
                o = nrm[:, j, ch(c)]
                m_nrm[c] = tt(P, o, o, rs, ALU.mult, m, m_hc)
            yield

        def front(i):
            s, c = chunks[i]
            k2 = i % 2
            if not s:
                yield from norm(c)
            DT, DU, XC, BCP = dt[k2], du[k2], xc[k2], bcp[k2]
            old = [last_exp[i - 2], last_mb[i - 2], *m_back[i - 2]] if i >= 2 else []
            t0 = c * T
            lo, hi = (max(t0 - 3, 0), t0 + T) if not s else (t0, min(t0 + T + 3, L))
            off = lo - (t0 - 3) if not s else 0
            n = hi - lo
            m_pad = []
            prev = [m_halo[i - 1]] if i else []
            if n < T + 3:
                z = xh[:, :, 0:3] if not s else xh[:, :, T:T + 3]
                m_pad = [fill(V, z, 0.0, *prev)]
            mx = {}
            for e in range(EJ):
                for j in range(CJ):
                    m = mm(PE, pw[:, 0:n], wx[:, j, e * 128:(e + 1) * 128], nrm[:, j, lo:hi],
                           j == 0, j == 1, m_nrm[c], *wb())
                mx[e] = w_free[0] = act(A, xh[:, e, off:off + n], pw[:, 0:n], ACT.Identity, m, *prev,
                                        bias=bxz[:, 0, e:e + 1])
                yield
            for e in range(EJ):
                for k in range(4):
                    o = 3 - k if s else k
                    m = mm(PE, pw[:, 0:T], diag[s][:, e, k, :], xh[:, e, o:o + T], k == 0, k == 3,
                           mx[e], *m_pad, *wb())
                m_halo[i] = m
                act(A, DU[:, e, :], pw[:, 0:T], ACT.Identity, m, *old, bias=vece[s][:, 0, e:e + 1])
                m = w_free[0] = act(A, DT[:, e, :], pw[:, 0:T], ACT.Relu, bias=vece[s][:, 3, e:e + 1])
                m = act(A, DT[:, e, :], DT[:, e, :], ACT.Exp, m, scale=-1.0, bias=CLAMP)
                yield
                m = act(A, DT[:, e, :], DT[:, e, :], ACT.Ln, m, bias=1.0)
                m = act(A, DT[:, e, :], DT[:, e, :], ACT.Exp, m, scale=-1.0)
                m_xc[i] = tt(V, XC[:, e, :], DU[:, e, :], DT[:, e, :], ALU.mult, m)
                yield
            for e in range(EJ):
                m = mm(PE, pw[:, 0:T], xpw[s][:, e, :], XC[:, e, :], e == 0, e == EJ - 1, m_xc[i], *wb())
            m1 = act(A, BCP[:, :], pw[:, 0:T], ACT.Copy, m, *([m_bc_done[i - 2]] if i >= 2 else []))
            m_r = act(A, res[0:R, :], pw[0:R, 0:T], ACT.Copy)
            m = w_free[0] = tt(V, res[64:128, :], pw[64:128, 0:T], BCP[64:128, :], ALU.subtract, m1, m_r)
            yield
            act(A, BCP[64:96, :], res[64:96, :], ACT.Copy, m)
            m = act(A, mid[96:128, :], res[96:128, :], ACT.Copy)
            m_bcp[i] = [m, tt(V, BCP[96:128, :], res[96:128, :], mid[96:128, :], ALU.subtract, m)]
            yield
            for e in range(EJ):
                m = mm(PE, pw[:, 0:T], wdt[s][:, e * 128:(e + 1) * 128], res[0:R, :], True, True, m_r, *wb())
                bias = vece[s][:, 1, e:e + 1]
                m2 = act(A, DT[:, e, :], pw[:, 0:T], ACT.Abs, m, m_xc[i], bias=bias)
                m3 = w_free[0] = act(A, DU[:, e, :], pw[:, 0:T], ACT.Relu, bias=bias)
                m = act(A, DT[:, e, :], DT[:, e, :], ACT.Exp, m2, scale=-1.0)
                m = act(A, DT[:, e, :], DT[:, e, :], ACT.Ln, m, bias=1.0)
                m = m_dt[i] = tt(V, DT[:, e, :], DT[:, e, :], DU[:, e, :], ALU.add, m, m3)
                m_du[i] = tt(V, DU[:, e, :], DT[:, e, :], XC[:, e, :], ALU.mult, m)
                yield

        def gate(i):
            s, c = chunks[i]
            mg = None
            for e in range(EJ):
                for j in range(CJ):
                    m = mm(PE, pw[:, 0:T], wz[:, j, e * 128:(e + 1) * 128], nrm[:, j, ch(c)],
                           j == 0, j == 1, *wb())
                free = [mg] if mg else ([m_gate[i - 1]] if i - 1 in m_gate else [])
                act(A, g1, pw[:, 0:T], ACT.Identity, m, *free, bias=bxz[:, 1, e:e + 1])
                m = w_free[0] = act(A, g2, pw[:, 0:T], ACT.Relu, bias=bxz[:, 2, e:e + 1])
                m = act(A, g2, g2, ACT.Exp, m, scale=-1.0, bias=CLAMP)
                yield
                m = act(A, g2, g2, ACT.Ln, m, bias=1.0)
                m = act(A, g2, g2, ACT.Exp, m, scale=-1.0)
                m = tt(V, g2, g1, g2, ALU.mult, m)
                mg = tt(V, yf[:, e, ch(c)], yf[:, e, ch(c)], g2, ALU.mult, m, m_back[i][e])
                yield
            m_gate[i] = mg
            for o in range(CJ):
                for e in range(EJ):
                    m = mm(PE, pw[0:CP, 0:T], wout[:, e, o * CP:(o + 1) * CP], yf[:, e, ch(c)],
                           e == 0, e == EJ - 1, mg, *wb())
                x = x1[:, o, ch(c)]
                m_out[c] = w_free[0] = stt(V, x, pw[0:CP, 0:T], vec0[:, 7, o:o + 1], x,
                                           ALU.add, ALU.add, m)
                yield

        m_gate, m_out, m_bc_done = {}, {}, {}
        U = [(i, n, e) for i in range(2 * NC) for n in range(NS) for e in range(EJ)]
        N = len(U)
        POOL_N = (3, 7, 11, 15)
        m_B, m_Bs, m_C, m_exp, m_mb, m_sc, m_mc, m_sum, m_car = ({} for _ in range(9))

        def bcast(i, n):
            g = (i * NS + n) * EJ
            w = i * NS + n
            prev = []
            if w >= 2:
                pi, pn = divmod(w - 2, NS)
                prev = [m_Bs[w - 2]] if pn in POOL_N else [m_mb[g - 4]]
            b = bbank[w % 2]
            m_B[w] = mm(PE, ps[:, b, 0:T], sel[:, n, :], bcp[i % 2][:, :], True, True, *m_bcp[i], *prev)
            if n in POOL_N:
                k = sum(1 for v in range(w) if v % NS in POOL_N)
                old = [m_mb[last_pool[-2]]] if len(last_pool) >= 2 else []
                m_Bs[w] = act(A, bs[:, k % 2, :], ps[:, b, 0:T], ACT.Copy, m_B[w], *old)
                last_pool.append(g + 2)
                slot_bs[w] = k % 2
            m = mm(PE, pw[:, 0:T], sel[:, NS + n, :], bcp[i % 2][:, :], True, True, *wb())
            m_bc_done[i] = m
            old = [m_mc[g - EJ * NCR + 2]] if w >= NCR else []
            m_C[w] = w_free[0] = act(A, cr[:, w % NCR, :], pw[:, 0:T], ACT.Copy, m, *old)

        last_pool, slot_bs = [], {}

        def mult_b(g, on_pool):
            i, n, e = U[g]
            if (n in POOL_N) != on_pool:
                return
            w = i * NS + n
            free = [m_sc[g - NDB]] if g >= NDB else []
            if on_pool:
                m = tt(P, db[:, g % NDB, :], du[i % 2][:, e, :], bs[:, slot_bs[w], :], ALU.mult,
                       m_Bs[w], m_du[i], *free)
            else:
                m = tt(V, db[:, g % NDB, :], du[i % 2][:, e, :], ps[:, bbank[w % 2], 0:T], ALU.mult,
                       m_B[w], m_du[i], *free)
            m_mb[g] = m
            last_mb[i] = m

        def decay(g):
            i, n, e = U[g]
            s = chunks[i][0]
            free = [m_sc[g - 2]] if g >= 2 else []
            m_exp[g] = act(A, ps[:, abank[g % 2], 0:T], dt[i % 2][:, e, :], ACT.Exp, m_dt[i], *free,
                           scale=Am[s][:, e, n:n + 1])
            last_exp[i] = m_exp[g]

        def step(g):
            i, n, e = U[g]
            s = chunks[i][0]
            init = 0.0 if i % NC == 0 else car[:, n, e:e + 1]
            free = [m_mc[g - NH]] if g >= NH else []
            if g >= NH:
                free.append(m_car[(g - NH) // EJ])
            m_sc[g] = scan(V, rev(hh[:, g % NH, :], s), rev(ps[:, abank[g % 2], 0:T], s),
                           rev(db[:, g % NDB, :], s), init, ALU.mult, ALU.add,
                           m_exp[g], m_mb[g], *free, *([m_car[(g - NS * EJ) // EJ]] if g >= NS * EJ else []))

        def carry(g):
            i, n, e = U[g]
            s = chunks[i][0]
            last = 0 if s else T - 1
            r = (g - 2) % NH
            m_car[g // EJ] = act(A, car[:, n, :], hh[:, r:r + EJ, last], ACT.Copy, m_sc[g])

        def mult_c(g):
            i, n, e = U[g]
            w = i * NS + n
            m_mc[g] = tt(P, pr[:, g % NPR, :], hh[:, g % NH, :], cr[:, w % NCR, :], ALU.mult,
                         m_sc[g], m_C[w], *([m_sum[g - NPR]] if g >= NPR else []))

        def total(g):
            i, n, e = U[g]
            free = [m_y1[i - 1][e]] if n == 0 and i else []
            m_sum[g] = mm(PE, ps[:, ybank[e], 0:T], ident[:, :], pr[:, g % NPR, :], n == 0, n == NS - 1,
                          m_mc[g], *free, inc=True)
            if n == NS - 1:
                s, c = chunks[i]
                y = ps[:, ybank[e], 0:T]
                o = yf[:, e, ch(c)]
                X, D = xc[i % 2][:, e, :], vece[s][:, 2, e:e + 1]
                if not s:
                    m = stt(V, o, X, D, y, ALU.mult, ALU.add, m_sum[g], m_nrm[c])
                    m_y1.setdefault(i, {})[e] = m
                else:
                    m = tt(V, o, o, y, ALU.add, m_sum[g])
                    m_y1.setdefault(i, {})[e] = m
                    m = stt(V, o, X, D, o, ALU.mult, ALU.add, m)
                m_back.setdefault(i, []).append(m)

        for _ in front(0):
            pass
        side = []
        bcast(0, 0)
        bcast(0, 1)
        for g in range(-4, N + 2):
            if 0 <= g < N and g % (NS * EJ) == 2:
                i = g // (NS * EJ)
                if i >= NC + 1:
                    side.append(gate(i - 1))
                if i + 1 < 2 * NC:
                    side.append(front(i + 1))
            if 0 <= g + 4 < N:
                mult_b(g + 4, True)
            if 0 <= g < N:
                step(g)
            if 0 <= g + 2 < N:
                mult_b(g + 2, False)
                decay(g + 2)
            w = (g + 5) // EJ
            if g >= 1 and (g - 1) % EJ == 0 and w < 2 * NC * NS:
                if w % NS == 0:
                    for x in side:
                        for _ in x:
                            pass
                    side = []
                bcast(*divmod(w, NS))
            if 0 <= g - 1 < N and (g - 1) % EJ == EJ - 1:
                carry(g - 1)
            if 0 <= g - 1 < N:
                mult_c(g - 1)
            if 0 <= g - 2 < N:
                total(g - 2)
            while side:
                try:
                    next(side[0])
                    break
                except StopIteration:
                    side.pop(0)
        for _ in gate(2 * NC - 1):
            pass
        return q, m_out

    def emit(blk, q):
        @blk.scalar
        def _(e):
            e.preload_act_table_set("natural_log_exp_and_others")
            q["a"].emit(e)

        @blk.vector
        def _(e):
            q["v"].emit(e)

        @blk.tensor
        def _(e):
            q["t"].emit(e)

    q0 = layer0()
    q1, m_out = layer1()
    nb = [sems["b" + e].num for e in "vapt"] + [s.num for s in s_ld]
    ncl = [sems["c" + e].num for e in "vaptd"]

    def clear(e, nums):
        for k in nums:
            e.sem_clear(range(k, k + 1))

    with nc.Fori(0, B) as b:
        xin = d["x"][bass.ds(b, 1)].rearrange("o (j p) n -> p (o j) n", p=CP)
        xout = d["out"][bass.ds(b, 1)].rearrange("o (j p) n -> p (o j) n", p=CP)
        with nc.Block() as blk:
            @blk.sync
            def _(e):
                for c in range(NC):
                    e.dma_start(x1[:, :, ch(c)], xin[:, :, ch(c)]).then_inc(s_ld[c], 16)
                for c in range(NC):
                    e.wait_ge(s_ld[c], 16)

            @blk.gpsimd
            def _(e):
                clear(e, ncl)
                q0["p"].emit(e)

            emit(blk, q0)
        with nc.Block() as blk:
            @blk.sync
            def _(e):
                for c in reversed(range(NC)):
                    e.wait_ge(m_out[c].sem, m_out[c].value)
                    e.dma_start(xout[:, :, ch(c)], x1[:, :, ch(c)]).then_inc(sems["cd"], 16)
                e.wait_ge(sems["cd"], 16 * NC)

            @blk.gpsimd
            def _(e):
                clear(e, nb)
                q1["p"].emit(e)

            emit(blk, q1)


def kernel(**inputs):
    import ml_dtypes
    import numpy as np
    import concourse.bacc as bacc
    from concourse.bass_utils import run_bass_kernel_spmd

    v = {k: np.asarray(a) for k, a in inputs.items()}
    l0, l1 = "L0_conv_", "L1_conv_"

    def wt(a, p):
        t = a.T
        return np.ascontiguousarray(t.reshape(t.shape[0] // p, p, t.shape[1]).transpose(1, 0, 2))

    def cols(names, p):
        return np.ascontiguousarray(np.stack([v[n].reshape(-1, p).T for n in names], axis=1))

    arrays = {
        "x": np.ascontiguousarray(v["x"].reshape(B, C, L)),
        "c_ident": np.eye(128, dtype=np.float32),
        "c_grp": np.kron(np.eye(CP // 6), np.ones((6, 6)) / 6).astype(np.float32),
        "c_ones": np.full((CP, CP), 1.0 / C, np.float32),
        "wk": wt(v[l0 + "Wk"], CP), "wv": wt(v[l0 + "Wv"], CP),
        "wr": wt(v[l0 + "Wr"], CP), "wo": wt(v[l0 + "Wo"], CP),
        "vec0": cols([l0 + "ln_g", l0 + "ln_b", l0 + "w_decay", l0 + "u"], CP),
        "b_out": cols([l1 + "b_out"], CP),
        "wx": wt(v[l1 + "W_in_x"], CP), "wz": wt(v[l1 + "W_in_z"], CP),
        "vec1": cols([l1 + "g1", l1 + "b1", l1 + "g2", l1 + "b2"], CP),
        "wout": wt(v[l1 + "W_out"], 128),
    }
    sel = np.zeros((128, 2 * NS, 128), np.float32)
    for part in range(1, 4):
        for n in range(2 * NS):
            sel[32 * part + n, n, :] = 1
    arrays["c_sel"] = sel.astype(ml_dtypes.bfloat16)
    for s, sfx in enumerate("fb"):
        w = wt(v[l1 + "W_xproj_" + sfx], 128)
        xp = np.zeros((128, EJ, 128), np.float32)
        xp[:, :, 0:R] = w[:, :, 0:R]
        for part in range(1, 4):
            xp[:, :, 32 * part:32 * part + 2 * NS] = w[:, :, R:]
        arrays[f"xpw{s}"] = xp
        arrays[f"wdt{s}"] = np.ascontiguousarray(v[l1 + "W_dt_" + sfx].T)
        arrays[f"alog{s}"] = np.ascontiguousarray(
            v[l1 + "A_log_" + sfx].reshape(EJ, 128, NS).transpose(1, 0, 2))
        arrays[f"vece{s}"] = cols([l1 + "conv_b_" + sfx, l1 + "dt_bias_" + sfx, l1 + "D_" + sfx], 128)
        arrays[f"tap{s}"] = np.ascontiguousarray(
            v[l1 + "conv_w_" + sfx].reshape(EJ, 128, 4).transpose(1, 0, 2).reshape(128, EJ * 4))

    nc = bacc.Bacc("TRN2", target_bir_lowering=False, num_devices=1)
    d = {k: nc.dram_tensor("in_" + k, a.shape, mybir.dt.from_np(a.dtype), kind="ExternalInput").ap()
         for k, a in arrays.items()}
    d["out"] = nc.dram_tensor("out_0", (B, C, L), F32, kind="ExternalOutput").ap()
    program(nc, d)
    r = run_bass_kernel_spmd(nc, [{"in_" + k: a for k, a in arrays.items()}], core_ids=[0])
    return r.results[0]["out_0"].reshape(B, C, 56, 56)
```

```python
from contextlib import ExitStack

import concourse.bass as bass
from concourse import mybir

F32 = mybir.dt.float32
BF16 = mybir.dt.bfloat16
ALU = mybir.AluOpType
ACT = mybir.ActivationFunctionType

B, C, L = 16, 192, 3136
CP, CJ = 96, 2
T, NC = 448, 7
EJ = 3
NS = 16
R = 12
CG = 3
CLAMP = 30.0


class Mark:

    def __init__(self, sem, value):
        self.sem, self.value = sem, value


class Queue:

    def __init__(self, sem):
        self.sem, self.count, self.ops = sem, 0, []

    def do(self, fn, *waits, inc=True):
        if inc:
            self.count += 1
        self.ops.append((fn, waits, inc))
        return Mark(self.sem, self.count)

    def emit(self, eng):
        seen = {}
        for fn, waits, inc in self.ops:
            for m in waits:
                if seen.get(m.sem.num, 0) < m.value:
                    eng.wait_ge(m.sem, m.value)
                    seen[m.sem.num] = m.value
            ins = fn(eng)
            if inc:
                ins.then_inc(self.sem, 1)


def tt(q, out, a, b, op, *w):
    return q.do(lambda e: e.tensor_tensor(out, a, b, op), *w)


def stt(q, out, a, s, b, op0, op1, *w):
    return q.do(lambda e: e.scalar_tensor_tensor(out, a, s, b, op0, op1), *w)


def ts(q, out, a, s1, s2, op0, op1, *w):
    return q.do(lambda e: e.tensor_scalar(out, a, s1, s2, op0, op1), *w)


def scan(q, out, a, b, init, op0, op1, *w):
    return q.do(lambda e: e.tensor_tensor_scan(out, a, b, init, op0, op1), *w)


def copy(q, out, a, *w):
    return q.do(lambda e: e.tensor_copy(out, a), *w)


def fill(q, out, v, *w):
    return q.do(lambda e: e.memset(out, v), *w)


def act(q, out, a, f, *w, bias=0.0, scale=1.0):
    return q.do(lambda e: e.activation(out, a, f, bias=bias, scale=scale), *w)


def mm(q, out, lhsT, rhs, start, stop, *w, inc=None):
    return q.do(lambda e: e.matmul(out, lhsT, rhs, start=start, stop=stop), *w,
                inc=stop if inc is None else inc)


def rev(ap, backward):
    return ap[:, ::-1] if backward else ap


def program(nc, d):
    with ExitStack() as ctx:
        build(nc, d, ctx)


def build(nc, d, ctx):
    def sb(name, shape, dt=F32):
        return ctx.enter_context(nc.sbuf_tensor(name, shape, dt))

    def sem(name):
        return ctx.enter_context(nc.semaphore(name))

    ident = sb("ident", [128, 128])
    grp = sb("grp", [CP, CP])
    ones = sb("ones", [CP, CP])
    sel = sb("sel", [128, 2 * NS, 128], BF16)
    w0 = {m: sb("w0" + m, [CP, CJ, C]) for m in "kvro"}
    vec0 = sb("vec0", [CP, 8, CJ])
    wx = sb("wx", [CP, CJ, 384])
    wz = sb("wz", [CP, CJ, 384])
    vec1 = sb("vec1", [CP, 4, CJ])
    wout = sb("wout", [128, EJ, C])
    bxz = sb("bxz", [128, 3, EJ])
    xpw = [sb(f"xpw{s}", [128, EJ, 128]) for s in range(2)]
    wdt = [sb(f"wdt{s}", [R, 384]) for s in range(2)]
    Am = [sb(f"A{s}", [128, EJ, NS]) for s in range(2)]
    diag = [sb(f"diag{s}", [128, EJ, 4, 128]) for s in range(2)]
    vece = [sb(f"vece{s}", [128, 4, EJ]) for s in range(2)]
    mv = sb("mv", [CP, CJ, 2])
    gs = sb("gs", [CP, 6, CJ])
    st = sb("st", [CP, CJ, NC, 6])
    eps = sb("eps", [128, 1])

    x1 = sb("x1", [CP, CJ, L])
    arena_n = 36016
    arena = sb("arena", [128, arena_n])
    ps = ctx.enter_context(nc.psum_tensor("ps", [128, 8, 512], F32))

    at = [0]

    def take(*shape, parts=128):
        n = 1
        for s in shape:
            n *= s
        o = at[0]
        at[0] += n
        assert at[0] <= arena_n, at[0]
        v = arena[0:parts, o:o + n]
        if len(shape) == 2:
            v = v.rearrange("p (a b) -> p a b", a=shape[0])
        elif len(shape) == 3:
            v = v.rearrange("p (a b c) -> p a b c", a=shape[0], b=shape[1])
        return v

    sems = {}
    for ph in "abc":
        for e in "vaptd":
            sems[ph + e] = sem(f"s_{ph}{e}")
    s_ld = [sem(f"s_ld{i}") for i in range(NC)]
    s_yw = [sem(f"s_yw{i}") for i in range(2)]
    s_yr = [sem(f"s_yr{i}") for i in range(2)]
    s_cw = [sem(f"s_cw{i}") for i in range(2)]
    s_cl = [sem(f"s_cl{i}") for i in range(CG)]
    cd = nc.dram_tensor("c_rows", (2, NS, T), F32, kind="Internal").ap()
    yd = nc.dram_tensor("y_forward", (NC, 128, EJ, T), F32, kind="Internal").ap()

    def queues(ph):
        return {e: Queue(sems[ph + e]) for e in "vapt"}

    q = queues("a")
    V, A, P, PE = q["v"], q["a"], q["p"], q["t"]
    loads = [
        (ident, d["c_ident"]), (grp, d["c_grp"]), (ones, d["c_ones"]), (sel, d["c_sel"]),
        (w0["k"], d["wk"]), (w0["v"], d["wv"]), (w0["r"], d["wr"]), (w0["o"], d["wo"]),
        (vec0[:, 0:4, :], d["vec0"]), (vec0[:, 7:8, :], d["b_out"]),
        (wx, d["wx"]), (wz, d["wz"]), (vec1, d["vec1"]), (wout, d["wout"]),
    ]
    for s in range(2):
        loads += [(xpw[s], d[f"xpw{s}"]), (wdt[s], d[f"wdt{s}"]), (Am[s], d[f"alog{s}"]),
                  (vece[s][:, 0:3, :], d[f"vece{s}"])]
    tap = take(2, EJ * 4)
    loads += [(tap[:, s, :], d[f"tap{s}"]) for s in range(2)]
    ld = Mark(sems["ad"], 16 * len(loads))

    m = act(A, vec0[:, 4, :], vec0[:, 2, :], ACT.Exp, ld)
    m = ts(V, vec0[:, 4, :], vec0[:, 4, :], -1.0, None, ALU.mult, ALU.bypass, m)
    m = tt(V, vec0[:, 5, :], vec0[:, 4, :], vec0[:, 3, :], ALU.add, ld, m)
    m = ts(V, vec0[:, 5, :], vec0[:, 5, :], 40.0, None, ALU.min, ALU.bypass, m)
    m = act(A, vec0[:, 5, :], vec0[:, 5, :], ACT.Exp, m)
    ts(V, vec0[:, 5, :], vec0[:, 5, :], -1.0, None, ALU.add, ALU.bypass, m)
    for o in range(CJ):
        for j in range(CJ):
            m_bo = mm(PE, ps[0:CP, 0, o:o + 1], w0["o"][:, j, o * CP:(o + 1) * CP],
                      vec0[:, 1, j:j + 1], j == 0, j == 1, ld)
    for i, (w, b) in enumerate(((wx, 1), (wz, 3))):
        for o in range(EJ):
            for j in range(CJ):
                m_bx = mm(PE, ps[:, 1 + i, o:o + 1], w[:, j, o * 128:(o + 1) * 128],
                          vec1[:, b, j:j + 1], j == 0, j == 1)
    copy(V, vec0[:, 6, :], ps[0:CP, 0, 0:CJ], m_bo)
    copy(V, bxz[:, 0, :], ps[:, 1, 0:EJ], m_bx)
    copy(V, bxz[:, 1, :], ps[:, 2, 0:EJ], m_bx)
    ts(V, bxz[:, 2, :], ps[:, 2, 0:EJ], CLAMP, None, ALU.add, ALU.bypass)
    for j in range(CJ):
        ts(V, w0["o"][:, j, :], w0["o"][:, j, :], vec0[:, 0, j:j + 1], None, ALU.mult, ALU.bypass, m_bo)
        ts(V, wx[:, j, :], wx[:, j, :], vec1[:, 0, j:j + 1], None, ALU.mult, ALU.bypass, m_bx)
        ts(V, wz[:, j, :], wz[:, j, :], vec1[:, 2, j:j + 1], None, ALU.mult, ALU.bypass, m_bx)
    fill(V, eps[:, :], 1e-5)
    for s in range(2):
        m = act(A, Am[s][:, :, :], Am[s][:, :, :], ACT.Exp, ld)
        ts(V, Am[s][:, :, :], Am[s][:, :, :], -1.0, None, ALU.mult, ALU.bypass, m)
        ts(V, vece[s][:, 3, :], vece[s][:, 0, :], CLAMP, None, ALU.add, ALU.bypass)
        for j in range(EJ):
            for k in range(4):
                ts(V, diag[s][:, j, k, :], ident[:, :], tap[:, s, 4 * j + k:4 * j + k + 1], None,
                   ALU.mult, ALU.bypass, ld)
    m_setup = [Mark(V.sem, V.count), Mark(A.sem, A.count)]

    with nc.Block() as blk:
        @blk.sync
        def _(e):
            for dst, src in loads:
                e.dma_start(dst[:], src).then_inc(sems["ad"], 16)
            for m in m_setup:
                e.wait_ge(m.sem, m.value)

        @blk.scalar
        def _(e):
            A.emit(e)

        @blk.vector
        def _(e):
            V.emit(e)

        @blk.tensor
        def _(e):
            PE.emit(e)

    def group_stats(V, A, PE, banks, after):
        dv, dv2, var = gs[:, 0, :], gs[:, 1, :], gs[:, 2, :]
        pm, pv = (ps[0:CP, b, 0:CJ] for b in banks)
        m1 = mm(PE, pm, grp[:, :], mv[:, :, 0], True, True, *after)
        m = tt(V, dv, mv[:, :, 0], pm, ALU.subtract, m1)
        m = tt(V, dv2, dv, dv, ALU.mult, m)
        m = tt(V, var, mv[:, :, 1], dv2, ALU.add, m)
        m = mm(PE, pv, grp[:, :], var, True, True, m)
        m = ts(V, gs[:, 3, :], pv, 1e-5, None, ALU.add, ALU.bypass, m)
        m = act(A, gs[:, 3, :], gs[:, 3, :], ACT.Ln, m)
        m = act(A, gs[:, 4, :], gs[:, 3, :], ACT.Exp, m, scale=-0.5)
        return stt(V, gs[:, 5, :], pm, -1.0, gs[:, 4, :], ALU.mult, ALU.mult, m)

    def ch(c):
        return slice(c * T, (c + 1) * T)

    def layer0():
        at[0] = 0
        q = queues("b")
        V, A, P, PE = q["v"], q["a"], q["p"], q["t"]
        xn = take(CJ, L, parts=CP)
        kk = take(CJ, L, parts=CP)
        vv = take(CJ, L, parts=CP)
        sg = take(CJ, L, parts=CP)
        Oc = take(3, T + 1, parts=CP)
        s1 = take(3, T, parts=CP)
        s2 = take(3, T, parts=CP)
        bv = take(3, T, parts=CP)
        pp = take(3, T, parts=CP)
        qq = take(3, T, parts=CP)
        lt = take(T, parts=CP)
        tn = take(2, T, parts=CP)

        for c in range(NC):
            for j in range(CJ):
                m = V.do(lambda e, c=c, j=j: e.bn_stats(st[:, j, c, :], x1[:, j, ch(c)]), Mark(s_ld[c], 16))
        for j in range(CJ):
            m2 = V.do(lambda e, j=j: e.bn_aggr(mv[:, j, :], st[:, j, :, :].rearrange("p a b -> p (a b)")), m)
        m_g = group_stats(V, A, PE, (0, 1), [m2])
        m_xn = {}
        for c in range(NC):
            for j in range(CJ):
                m_xn[c] = ts(V, xn[:, j, ch(c)], x1[:, j, ch(c)], gs[:, 4, j:j + 1], gs[:, 5, j:j + 1],
                             ALU.mult, ALU.add, m_g)

        bank_free = [None] * 8
        nb = [0]

        def bank():
            i = 2 + nb[0] % 6
            nb[0] += 1
            return i, [bank_free[i]] if bank_free[i] else []

        m_kv = {}

        def project(c):
            for j in range(CJ):
                for name, dst in (("k", kk), ("v", vv), ("r", sg)):
                    b, free = bank()
                    out = ps[0:CP, b, 0:T]
                    for i in range(CJ):
                        m = mm(PE, out, w0[name][:, i, j * CP:(j + 1) * CP], xn[:, i, ch(c)],
                               i == 0, i == 1, m_xn[c], *free)
                    o = dst[:, j, ch(c)]
                    if name == "r":
                        m = act(A, o, out, ACT.Relu, m, bias=CLAMP)
                        bank_free[b] = m
                        m = act(A, o, o, ACT.Exp, m, scale=-1.0, bias=CLAMP)
                        m = act(A, o, o, ACT.Ln, m, bias=1.0)
                        m_kv[name, c, j] = act(A, o, o, ACT.Exp, m, scale=-1.0)
                    else:
                        m_kv[name, c, j] = bank_free[b] = act(A, o, out, ACT.Copy, m)

        units = [(0, c, j) for c in range(NC) for j in range(CJ)]
        units += [(1, c, j) for c in reversed(range(NC)) for j in range(CJ)]
        mO, ms, mB, mP, mN, mD, mR, mT, mY = ({} for _ in range(9))

        def stage1(u):
            s, c, j = units[u]
            r = u % 3
            first = c == (NC - 1 if s else 0)
            edge = T if s else 0
            cur = Oc[:, r, 0:T] if s else Oc[:, r, 1:T + 1]
            prv = Oc[:, r, 1:T + 1] if s else Oc[:, r, 0:T]
            free = [ms[u - 3]] if u >= 3 else []
            if first:
                m = fill(V, Oc[:, r, edge:edge + 1], -1e38, *free)
                init = -1e38
            else:
                ro = (u - 2) % 3
                last = 0 if s else T
                m = copy(V, Oc[:, r, edge:edge + 1], Oc[:, ro, last:last + 1], mO[u - 2], *free)
                init = Oc[:, ro, last:last + 1]
            mO[u] = scan(V, rev(cur, s), vec0[:, 4, j:j + 1].to_broadcast([CP, T]), rev(kk[:, j, ch(c)], s),
                         init, ALU.add, ALU.max, m_kv["k", c, j], m)
            free = [mT[u - 3], mD[u - 3]] if u >= 3 else []
            m1 = tt(P, s1[:, r, :], prv, cur, ALU.subtract, mO[u], *free)
            m2 = ms[u] = tt(P, s2[:, r, :], kk[:, j, ch(c)], cur, ALU.subtract)
            act(A, s1[:, r, :], s1[:, r, :], ACT.Exp, m1, bias=vec0[:, 4, j:j + 1])
            mB[u] = act(A, s2[:, r, :], s2[:, r, :], ACT.Exp, m2)

        def stage2(u):
            s, c, j = units[u]
            r = u % 3
            first = c == (NC - 1 if s else 0)
            ro, last = (u - 2) % 3, 0 if s else T - 1
            free = [mY[u - 3]] if u >= 3 else []
            m = tt(V, bv[:, r, :], s2[:, r, :], vv[:, j, ch(c)], ALU.mult, mB[u], m_kv["v", c, j], *free)
            prev = [mP[u - 2]] if not first else []
            i0 = 0.0 if first else pp[:, ro, last:last + 1]
            i1 = 0.0 if first else qq[:, ro, last:last + 1]
            m0 = scan(V, rev(pp[:, r, :], s), rev(s1[:, r, :], s), rev(bv[:, r, :], s), i0,
                      ALU.mult, ALU.add, m, *prev)
            m1 = mP[u] = scan(V, rev(qq[:, r, :], s), rev(s1[:, r, :], s), rev(s2[:, r, :], s), i1,
                              ALU.mult, ALU.add)
            mN[u] = stt(V, bv[:, r, :], bv[:, r, :], vec0[:, 5, j:j + 1], pp[:, r, :], ALU.mult, ALU.add, m0)
            m = stt(V, s2[:, r, :], s2[:, r, :], vec0[:, 5, j:j + 1], qq[:, r, :], ALU.mult, ALU.add, m1)
            m = act(A, lt, s2[:, r, :], ACT.Ln, m, *([mR[u - 1]] if u else []))
            m = mR[u] = act(A, s1[:, r, :], lt, ACT.Exp, m, scale=-1.0)
            mD[u] = tt(P, tn[:, u % 2, :], s2[:, r, :], s1[:, r, :], ALU.mult, m,
                       *([mY[u - 2]] if u >= 2 else []))

        m_add = {}

        def stage3(u):
            s, c, j = units[u]
            r = u % 3
            t = tn[:, u % 2, :]
            m = mT[u] = stt(V, t, t, 2.0, s1[:, r, :], ALU.subtract, ALU.mult, mD[u])
            ya = xn[:, j, ch(c)]
            if not s:
                mY[u] = m_add[c, j] = tt(V, ya, bv[:, r, :], t, ALU.mult, m, mN[u], m_kv["r", c, CJ - 1])
            else:
                m = tt(V, t, bv[:, r, :], t, ALU.mult, m, mN[u])
                mY[u] = m_add[c, j] = tt(P, ya, ya, t, ALU.add, m, m_add[c, j])

        def finish(c):
            m = None
            for j in range(CJ):
                h = xn[:, j, ch(c)]
                m = stt(V, h, h, -0.5, sg[:, j, ch(c)], ALU.mult, ALU.mult, m_add[c, j], m_kv["r", c, j])
            b, free = bank()
            mean = ps[0:CP, b, 0:T]
            for j in range(CJ):
                m1 = mm(PE, mean, ones[:, :], xn[:, j, ch(c)], j == 0, j == 1, m, *free)
            for j in range(CJ):
                h = xn[:, j, ch(c)]
                m = tt(V, h, h, mean, ALU.subtract, m1)
                m2 = act(A, sg[:, j, ch(c)], h, ACT.Square, m)
            bank_free[b] = m_hc = m
            b, free = bank()
            var = ps[0:CP, b, 0:T]
            for j in range(CJ):
                m = mm(PE, var, ones[:, :], sg[:, j, ch(c)], j == 0, j == 1, m2, *free)
            rs = kk[:, 0, ch(c)]
            m = ts(V, rs, var, 1e-5, None, ALU.add, ALU.bypass, m)
            bank_free[b] = m
            m = act(A, rs, rs, ACT.Ln, m)
            m = act(A, rs, rs, ACT.Exp, m, scale=-0.5)
            for j in range(CJ):
                h = xn[:, j, ch(c)]
                m1 = tt(P, h, h, rs, ALU.mult, m, m_hc)
            for o in range(CJ):
                b, free = bank()
                out = ps[0:CP, b, 0:T]
                for j in range(CJ):
                    m = mm(PE, out, w0["o"][:, j, o * CP:(o + 1) * CP], xn[:, j, ch(c)],
                           j == 0, j == 1, m1, *free)
                x = x1[:, o, ch(c)]
                m = bank_free[b] = stt(V, x, out, vec0[:, 6, o:o + 1], x, ALU.add, ALU.add, m)
                V.do(lambda e, c=c, o=o: e.bn_stats(st[:, o, c, :], x1[:, o, ch(c)]), m)

        n = len(units)
        project(0)
        for u in range(n + 3):
            if u < n:
                if u % 2 == 0 and u // 2 + 1 < NC:
                    project(u // 2 + 1)
                stage1(u)
            if 1 <= u <= n:
                stage2(u - 1)
            if 2 <= u <= n + 1:
                stage3(u - 2)
            if u >= n // 2 + 4 and (u - n // 2) % 2 == 0:
                finish(units[u - 4][1])
        m = Mark(V.sem, V.count)
        for j in range(CJ):
            V.do(lambda e, j=j: e.bn_aggr(mv[:, j, :], st[:, j, :, :].rearrange("p a b -> p (a b)")), m)
        return q

    def layer1():
        at[0] = 0
        q = queues("c")
        V, A, P, PE = q["v"], q["a"], q["p"], q["t"]
        nrm = take(CJ, L, parts=CP)
        yb = [take(EJ, T) for _ in range(2)]
        tmp = take(3, T)
        xh = take(EJ, T + 3)
        mid = xh[:, 0, 0:T // 2].bitcast(BF16)
        xc = [take(EJ, T) for _ in range(2)]
        dt = [take(EJ, T) for _ in range(2)]
        du = [take(EJ, T) for _ in range(2)]
        bcp = [take(T // 2).bitcast(BF16) for _ in range(2)]
        res = take(T)
        NDB, NH, NPR = 6, 6, 5
        cr = take(CG * 4, T)
        bs = take(T)
        db = take(NDB, T)
        hh = take(NH, T)
        pr = take(NPR, T)
        g1, g2 = tmp[:, 0, :], tmp[:, 1, :]
        car = take(NS, EJ)
        ybank, abank, bbank, wbank = (0, 1, 2), (3, 4), (5, 6), 7

        w_free = {wbank: []}

        def w_take():
            return wbank, ps[:, wbank, 0:T], w_free.pop(wbank)

        m_g = group_stats(V, A, PE, (5, 6), [])
        m_nrm, m_xc, m_dt, m_du, m_bcp, m_halo = {}, {}, {}, {}, {}, {}
        last_exp, last_mb, m_back, m_y1 = {}, {}, {}, {}
        chunks = [(0, c) for c in range(NC)] + [(1, c) for c in reversed(range(NC))]

        def norm(c):
            for j in range(CJ):
                m = ts(V, nrm[:, j, ch(c)], x1[:, j, ch(c)], gs[:, 4, j:j + 1], gs[:, 5, j:j + 1],
                       ALU.mult, ALU.add, m_g)
            yield
            b, pw, free = w_take()
            for j in range(CJ):
                if j:
                    yield
                m1 = mm(PE, pw[0:CP, :], ones[:, :], nrm[:, j, ch(c)], j == 0, j == 1, m, *free)
            yield
            for j in range(CJ):
                o = nrm[:, j, ch(c)]
                m = m_hc = tt(V, o, o, pw[0:CP, :], ALU.subtract, m1)
            w_free[b] = [m]
            yield
            for j in range(CJ):
                sq = act(A, tmp[0:CP, j, :], nrm[:, j, ch(c)], ACT.Square, m, *([m_nrm[c - 1]] if c else []))
            yield
            b, pw, free = w_take()
            for j in range(CJ):
                if j:
                    yield
                m = mm(PE, pw[0:CP, :], ones[:, :], tmp[0:CP, j, :], j == 0, j == 1, sq, *free)
            rs = tmp[0:CP, 2, :]
            yield
            m = act(A, rs, pw[0:CP, :], ACT.Ln, m, bias=eps[0:CP, :])
            w_free[b] = [m]
            m = act(A, rs, rs, ACT.Exp, m, scale=-0.5)
            yield
            for j in range(CJ):
                o = nrm[:, j, ch(c)]
                m_nrm[c] = tt(P, o, o, rs, ALU.mult, m, m_hc)
            yield

        def front(i):
            s, c = chunks[i]
            k2 = i % 2
            if not s:
                yield from norm(c)
            DT, DU, XC, BCP = dt[k2], du[k2], xc[k2], bcp[k2]
            old = [last_exp[i - 2], last_mb[i - 2], *m_back[i - 2]] if i >= 2 else []
            t0 = c * T
            lo, hi = (max(t0 - 3, 0), t0 + T) if not s else (t0, min(t0 + T + 3, L))
            off = lo - (t0 - 3) if not s else 0
            n = hi - lo
            m_pad = []
            prev = [m_halo[i - 1]] if i else []
            if n < T + 3:
                z = xh[:, :, 0:3] if not s else xh[:, :, T:T + 3]
                m_pad = [fill(V, z, 0.0, *prev)]
            mx = {}
            for e in range(EJ):
                b, pw, free = w_take()
                pw = ps[:, b, 0:n]
                for j in range(CJ):
                    if j:
                        yield
                    m = mm(PE, pw, wx[:, j, e * 128:(e + 1) * 128], nrm[:, j, lo:hi],
                           j == 0, j == 1, m_nrm[c], *free)
                yield
                mx[e] = act(A, xh[:, e, off:off + n], pw, ACT.Identity, m, *prev,
                            bias=bxz[:, 0, e:e + 1])
                w_free[b] = [mx[e]]
            m_e, m_z = {}, {}
            for e in range(EJ + 2):
                if e < EJ:
                    b, pw, free = w_take()
                    for k in range(4):
                        if k:
                            yield
                        o = 3 - k if s else k
                        m = mm(PE, pw, diag[s][:, e, k, :], xh[:, e, o:o + T], k == 0, k == 3,
                               mx[e], *m_pad, *free)
                    m_halo[i] = m
                if 1 <= e <= EJ:
                    m_e[e - 1] = act(A, DT[:, e - 1, :], DT[:, e - 1, :], ACT.Ln, m_e[e - 1], bias=1.0)
                    m_e[e - 1] = act(A, DT[:, e - 1, :], DT[:, e - 1, :], ACT.Exp, m_e[e - 1], scale=-1.0)
                yield
                if e < EJ:
                    m_z[e] = act(A, DU[:, e, :], pw, ACT.Identity, m, *old, bias=vece[s][:, 0, e:e + 1])
                    m = act(A, DT[:, e, :], pw, ACT.Relu, bias=vece[s][:, 3, e:e + 1])
                    w_free[b] = [m]
                    m_e[e] = act(A, DT[:, e, :], DT[:, e, :], ACT.Exp, m, scale=-1.0, bias=CLAMP)
                if e >= 2:
                    m_xc[i] = tt(V, XC[:, e - 2, :], DU[:, e - 2, :], DT[:, e - 2, :], ALU.mult,
                                 m_e[e - 2], m_z[e - 2])
                yield
            b, pw, free = w_take()
            for e in range(EJ):
                if e:
                    yield
                m = mm(PE, pw, xpw[s][:, e, :], XC[:, e, :], e == 0, e == EJ - 1, m_xc[i], *free)
            yield
            m1 = act(A, BCP[:, :], pw, ACT.Copy, m, *([m_bc_done[i - 2]] if i >= 2 else []))
            m_c = act(A, res[32:64, :], pw[32:64, :], ACT.Copy,
                      *([Mark(s_cw[(i - 1) % 2], 16 * ((i - 1) // 2 + 1))] if i else []))
            m_r = act(A, res[0:R, :], pw[0:R, :], ACT.Copy)
            read = [m_cload[G] for G in range(4 * i - 8, 4 * i - 4)] if i >= 2 else []
            sp.append(([m_c, *read], cd[i % 2], res[48:64, :], s_cw[i % 2]))
            yield
            m = tt(V, res[64:128, :], pw[64:128, :], BCP[64:128, :], ALU.subtract, m1, m_r)
            w_free[b] = [m]
            yield
            act(A, BCP[64:96, :], res[64:96, :], ACT.Copy, m)
            m1 = act(A, mid[96:128, :], res[96:128, :], ACT.Copy, m_halo[i])
            yield
            m_bcp[i] = [m1, tt(V, BCP[96:128, :], res[96:128, :], mid[96:128, :], ALU.subtract, m1)]
            m2, m3, m4 = {}, {}, {}
            for e in range(EJ + 2):
                if e < EJ:
                    b, pw, free = w_take()
                    m = mm(PE, pw, wdt[s][:, e * 128:(e + 1) * 128], res[0:R, :], True, True, m_r, *free)
                if e >= 2:
                    m_dt[i] = tt(V, DT[:, e - 2, :], DT[:, e - 2, :], DU[:, e - 2, :], ALU.add,
                                 m4[e - 2], m3[e - 2])
                yield
                if e < EJ:
                    bias = vece[s][:, 1, e:e + 1]
                    m2[e] = act(A, DT[:, e, :], pw, ACT.Abs, m, m_xc[i], bias=bias)
                    m3[e] = act(A, DU[:, e, :], pw, ACT.Relu, bias=bias)
                    w_free[b] = [m3[e]]
                    m4[e] = act(A, DT[:, e, :], DT[:, e, :], ACT.Exp, m2[e], scale=-1.0)
                if 1 <= e <= EJ:
                    m4[e - 1] = act(A, DT[:, e - 1, :], DT[:, e - 1, :], ACT.Ln, m4[e - 1], bias=1.0)
                if e >= 2:
                    m_du[i] = tt(P, DU[:, e - 2, :], DT[:, e - 2, :], XC[:, e - 2, :], ALU.mult, m_dt[i])
                yield

        def gate(i):
            s, c = chunks[i]
            mg = None
            for e in range(EJ):
                b, pw, free = w_take()
                for j in range(CJ):
                    if j:
                        yield
                    m = mm(PE, pw, wz[:, j, e * 128:(e + 1) * 128], nrm[:, j, ch(c)],
                           j == 0, j == 1, *free)
                yield
                free = [mg] if mg else ([m_gate[i - 1]] if i - 1 in m_gate else [])
                act(A, g1, pw, ACT.Identity, m, *free, bias=bxz[:, 1, e:e + 1])
                m = act(A, g2, pw, ACT.Relu, bias=bxz[:, 2, e:e + 1])
                w_free[b] = [m]
                m = act(A, g2, g2, ACT.Exp, m, scale=-1.0, bias=CLAMP)
                yield
                m = act(A, g2, g2, ACT.Ln, m, bias=1.0)
                m = act(A, g2, g2, ACT.Exp, m, scale=-1.0)
                yield
                m = tt(P, g2, g1, g2, ALU.mult, m)
                yield
                mg = tt(P, yb[i % 2][:, e, :], yb[i % 2][:, e, :], g2, ALU.mult, m, m_back[i][e])
                yield
            m_gate[i] = mg
            for o in range(CJ):
                b, pw, free = w_take()
                pw = pw[0:CP, :]
                for e in range(EJ):
                    if e:
                        yield
                    m = mm(PE, pw, wout[:, e, o * CP:(o + 1) * CP], yb[i % 2][:, e, :],
                           e == 0, e == EJ - 1, mg, *free)
                yield
                x = x1[:, o, ch(c)]
                m_gated[i] = m
                m_out[c] = stt(V, x, pw, vec0[:, 7, o:o + 1], x, ALU.add, ALU.add, m)
                w_free[b] = [m_out[c]]
                yield
            if i + 2 < 2 * NC:
                load_y(i + 2)
            sp.append(([m_out[c]], ch(c), None, sems["cd"]))

        m_gate, m_out, m_bc_done, m_gated, m_cload, sp = {}, {}, {}, {}, {}, []
        U = [(i, n, e) for i in range(2 * NC) for n in range(NS) for e in range(EJ)]
        N = len(U)
        POOL_N = (3, 7, 11, 15)
        LC, LT, LM, LB = 1, 3, 3, 5
        m_B, m_Bs, m_C, m_exp, m_mb, m_sc, m_mc, m_sum, m_car = ({} for _ in range(9))

        def bcast_b(i, n):
            w = i * NS + n
            prev = []
            if w >= 2:
                prev = [m_Bs[w - 2]] if (n - 2) % NS in POOL_N else [m_mb[w * EJ - 4]]
            b = bbank[w % 2]
            m_B[w] = m_bc_done[i] = mm(PE, ps[:, b, 0:T], sel[:, n, :], bcp[i % 2][:, :], True, True,
                                       *m_bcp[i], *prev)
            if n in POOL_N:
                old = [m_mb[last_pool[-1]]] if last_pool else []
                m_Bs[w] = act(A, bs[:, :], ps[:, b, 0:T], ACT.Copy, m_B[w], *old)
                last_pool.append(w * EJ + 2)

        def load_c(G):
            i, n = divmod(4 * G, NS)
            k = G % CG
            free = [m_mc[(4 * (G - CG) + 4) * EJ - 1]] if G >= CG else []
            src = cd[i % 2, n:n + 4, :].unsqueeze(0).to_broadcast([128, 4, T])
            sp.append(([Mark(s_cw[i % 2], 16 * (i // 2 + 1)), *free], cr[:, 4 * k:4 * k + 4, :], src, s_cl[k]))
            m_cload[G] = Mark(s_cl[k], 16 * (G // CG + 1))

        def load_y(i):
            c = chunks[i][1]
            w = [Mark(s_yw[b], 16 * sum(1 for k in range(NC) if k % 2 == b)) for b in range(2)]
            if i - 2 >= NC:
                w.append(m_gated[i - 2])
            sp.append((w, yb[i % 2], yd[c], s_yr[i % 2]))

        last_pool = []

        def mult_b(g, on_pool):
            i, n, e = U[g]
            if (n in POOL_N) != on_pool:
                return
            w = i * NS + n
            free = [m_sc[g - NDB]] if g >= NDB else []
            if on_pool:
                m = tt(P, db[:, g % NDB, :], du[i % 2][:, e, :], bs[:, :], ALU.mult,
                       m_Bs[w], m_du[i], *free)
            else:
                m = tt(V, db[:, g % NDB, :], du[i % 2][:, e, :], ps[:, bbank[w % 2], 0:T], ALU.mult,
                       m_B[w], m_du[i], *free)
            m_mb[g] = m
            last_mb[i] = m

        def decay(g):
            i, n, e = U[g]
            s = chunks[i][0]
            free = [m_sc[g - 2]] if g >= 2 else []
            m_exp[g] = act(A, ps[:, abank[g % 2], 0:T], dt[i % 2][:, e, :], ACT.Exp, m_dt[i], *free,
                           scale=Am[s][:, e, n:n + 1])
            last_exp[i] = m_exp[g]

        def step(g):
            i, n, e = U[g]
            s = chunks[i][0]
            init = 0.0 if i % NC == 0 else car[:, n, e:e + 1]
            free = [m_mc[g - NH]] if g >= NH else []
            if g >= NH:
                free.append(m_car[(g - NH) // EJ])
            m_sc[g] = scan(V, rev(hh[:, g % NH, :], s), rev(ps[:, abank[g % 2], 0:T], s),
                           rev(db[:, g % NDB, :], s), init, ALU.mult, ALU.add,
                           m_exp[g], m_mb[g], *free, *([m_car[(g - NS * EJ) // EJ]] if g >= NS * EJ else []))

        def carry(g):
            i, n, e = U[g]
            s = chunks[i][0]
            last = 0 if s else T - 1
            r = (g - 2) % NH
            m_car[g // EJ] = act(A, car[:, n, :], hh[:, r:r + EJ, last], ACT.Copy, m_sc[g])

        def mult_c(g):
            i, n, e = U[g]
            w = i * NS + n
            m_mc[g] = tt(P, pr[:, g % NPR, :], hh[:, g % NH, :], cr[:, w % (4 * CG), :], ALU.mult,
                         m_sc[g], m_cload[w // 4], *([m_sum[g - NPR]] if g >= NPR else []))

        def total(g):
            i, n, e = U[g]
            free = [m_y1[i - 1][e]] if n == 0 and i else []
            m_sum[g] = mm(PE, ps[:, ybank[e], 0:T], ident[:, :], pr[:, g % NPR, :], n == 0, n == NS - 1,
                          m_mc[g], *free, inc=True)
            if n == NS - 1:
                s, c = chunks[i]
                y = ps[:, ybank[e], 0:T]
                o = yb[i % 2][:, e, :]
                X, D = xc[i % 2][:, e, :], vece[s][:, 2, e:e + 1]
                if not s:
                    free = [Mark(s_yw[i % 2], 16 * (i // 2))] if i >= 2 else []
                    m = stt(V, o, X, D, y, ALU.mult, ALU.add, m_sum[g], *free)
                    m_y1.setdefault(i, {})[e] = m
                else:
                    m = tt(V, o, o, y, ALU.add, m_sum[g], Mark(s_yr[i % 2], 16 * ((i - NC) // 2 + 1)))
                    m_y1.setdefault(i, {})[e] = m
                    m = stt(V, o, X, D, o, ALU.mult, ALU.add, m)
                m_back.setdefault(i, []).append(m)
                if e == EJ - 1:
                    if not s:
                        sp.append((m_back[i], yd[i], yb[i % 2], s_yw[i % 2]))
                    if i == NC - 1:
                        load_y(NC)
                        load_y(NC + 1)

        for _ in front(0):
            pass
        NW = 2 * NC * NS
        fronts, gates, waiting = [], [], []

        def side():
            for lst in (fronts, gates):
                while lst:
                    try:
                        next(lst[0])
                        return
                    except StopIteration:
                        lst.pop(0)

        for G in range(CG):
            load_c(G)
        for g in range(-LB, N + LT):
            w, r = divmod(g + LB, EJ)
            if r == 0 and w < NW:
                if w % NS == 0:
                    for x in fronts:
                        for _ in x:
                            pass
                    fronts.clear()
                bcast_b(w // NS, w % NS)
            if 0 <= g < N and g % (NS * EJ) == LT:
                i = g // (NS * EJ)
                if i >= NC + 1:
                    gates.append(gate(i - 1))
                if i + 1 < 2 * NC:
                    fronts.append(front(i + 1))
            if 0 <= g < N:
                step(g)
            if 0 <= g + LM < N:
                mult_b(g + LM, False)
            if 0 <= g + 3 < N:
                mult_b(g + 3, True)
            if 0 <= g + 2 < N:
                decay(g + 2)
            if 0 <= g - 1 < N and (g - 1) % EJ == EJ - 1:
                carry(g - 1)
            if 0 <= g - LC < N:
                mult_c(g - LC)
                G = (g - LC) // (4 * EJ)
                if (g - LC) % (4 * EJ) == 4 * EJ - 1 and 4 * (G + CG) < NW:
                    waiting.append(G + CG)
            while waiting and 4 * waiting[0] // NS in m_bcp:
                load_c(waiting.pop(0))
            if 0 <= g - LT < N:
                total(g - LT)
            side()
            if g % 2:
                side()
        for x in gates:
            for _ in x:
                pass
        for _ in gate(2 * NC - 1):
            pass
        return q, sp

    def emit(blk, q):
        @blk.scalar
        def _(e):
            e.preload_act_table_set("natural_log_exp_and_others")
            q["a"].emit(e)

        @blk.vector
        def _(e):
            q["v"].emit(e)

        @blk.tensor
        def _(e):
            q["t"].emit(e)

    q0 = layer0()
    q1, sp1 = layer1()
    nb = [sems["b" + e].num for e in "vapt"] + [s.num for s in s_ld]
    ncl = [sems["c" + e].num for e in "vaptd"] + [s.num for s in s_yw + s_yr + s_cw + s_cl]

    def clear(e, nums):
        for k in nums:
            e.sem_clear(range(k, k + 1))

    with nc.Fori(0, B) as b:
        xin = d["x"][bass.ds(b, 1)].rearrange("o (j p) n -> p (o j) n", p=CP)
        xout = d["out"][bass.ds(b, 1)].rearrange("o (j p) n -> p (o j) n", p=CP)
        with nc.Block() as blk:
            @blk.sync
            def _(e):
                for c in range(NC):
                    e.dma_start(x1[:, :, ch(c)], xin[:, :, ch(c)]).then_inc(s_ld[c], 16)
                for c in range(NC):
                    e.wait_ge(s_ld[c], 16)

            @blk.gpsimd
            def _(e):
                clear(e, ncl)
                q0["p"].emit(e)

            emit(blk, q0)
        with nc.Block() as blk:
            @blk.sync
            def _(e):
                for waits, dst, src, done in sp1:
                    for m in waits:
                        e.wait_ge(m.sem, m.value)
                    if src is None:
                        dst, src = xout[:, :, dst], x1[:, :, dst]
                    e.dma_start(dst, src).then_inc(done, 16)
                e.wait_ge(sems["cd"], 16 * NC)

            @blk.gpsimd
            def _(e):
                clear(e, nb)
                q1["p"].emit(e)

            emit(blk, q1)


def kernel(**inputs):
    import ml_dtypes
    import numpy as np
    import concourse.bacc as bacc
    from concourse.bass_utils import run_bass_kernel_spmd

    v = {k: np.asarray(a) for k, a in inputs.items()}
    l0, l1 = "L0_conv_", "L1_conv_"

    def wt(a, p):
        t = a.T
        return np.ascontiguousarray(t.reshape(t.shape[0] // p, p, t.shape[1]).transpose(1, 0, 2))

    def cols(names, p):
        return np.ascontiguousarray(np.stack([v[n].reshape(-1, p).T for n in names], axis=1))

    arrays = {
        "x": np.ascontiguousarray(v["x"].reshape(B, C, L)),
        "c_ident": np.eye(128, dtype=np.float32),
        "c_grp": np.kron(np.eye(CP // 6), np.ones((6, 6)) / 6).astype(np.float32),
        "c_ones": np.full((CP, CP), 1.0 / C, np.float32),
        "wk": wt(v[l0 + "Wk"], CP), "wv": wt(v[l0 + "Wv"], CP),
        "wr": wt(v[l0 + "Wr"], CP), "wo": wt(v[l0 + "Wo"], CP),
        "vec0": cols([l0 + "ln_g", l0 + "ln_b", l0 + "w_decay", l0 + "u"], CP),
        "b_out": cols([l1 + "b_out"], CP),
        "wx": wt(v[l1 + "W_in_x"], CP), "wz": wt(v[l1 + "W_in_z"], CP),
        "vec1": cols([l1 + "g1", l1 + "b1", l1 + "g2", l1 + "b2"], CP),
        "wout": wt(v[l1 + "W_out"], 128),
    }
    sel = np.zeros((128, 2 * NS, 128), np.float32)
    for part in range(1, 4):
        for n in range(2 * NS):
            sel[32 * part + n, n, :] = 1
    arrays["c_sel"] = sel.astype(ml_dtypes.bfloat16)
    for s, sfx in enumerate("fb"):
        w = wt(v[l1 + "W_xproj_" + sfx], 128)
        xp = np.zeros((128, EJ, 128), np.float32)
        xp[:, :, 0:R] = w[:, :, 0:R]
        for part in range(1, 4):
            xp[:, :, 32 * part:32 * part + 2 * NS] = w[:, :, R:]
        arrays[f"xpw{s}"] = xp
        arrays[f"wdt{s}"] = np.ascontiguousarray(v[l1 + "W_dt_" + sfx].T)
        arrays[f"alog{s}"] = np.ascontiguousarray(
            v[l1 + "A_log_" + sfx].reshape(EJ, 128, NS).transpose(1, 0, 2))
        arrays[f"vece{s}"] = cols([l1 + "conv_b_" + sfx, l1 + "dt_bias_" + sfx, l1 + "D_" + sfx], 128)
        arrays[f"tap{s}"] = np.ascontiguousarray(
            v[l1 + "conv_w_" + sfx].reshape(EJ, 128, 4).transpose(1, 0, 2).reshape(128, EJ * 4))

    nc = bacc.Bacc("TRN2", target_bir_lowering=False, num_devices=1)
    d = {k: nc.dram_tensor("in_" + k, a.shape, mybir.dt.from_np(a.dtype), kind="ExternalInput").ap()
         for k, a in arrays.items()}
    d["out"] = nc.dram_tensor("out_0", (B, C, L), F32, kind="ExternalOutput").ap()
    program(nc, d)
    r = run_bass_kernel_spmd(nc, [{"in_" + k: a for k, a in arrays.items()}], core_ids=[0])
    return r.results[0]["out_0"].reshape(B, C, 56, 56)
```

```python
from contextlib import ExitStack

import concourse.bass as bass
from concourse import mybir

F32 = mybir.dt.float32
BF16 = mybir.dt.bfloat16
ALU = mybir.AluOpType
ACT = mybir.ActivationFunctionType

B, C, L = 16, 192, 3136
CP, CJ = 96, 2
T, NC = 448, 7
EJ = 3
NS = 16
R = 12
CG = 3
CLAMP = 30.0


class Mark:

    def __init__(self, sem, value):
        self.sem, self.value = sem, value


class Queue:

    def __init__(self, sem):
        self.sem, self.count, self.ops = sem, 0, []

    def do(self, fn, *waits, inc=True):
        if inc:
            self.count += 1
        self.ops.append((fn, waits, inc))
        return Mark(self.sem, self.count)

    def emit(self, eng):
        seen = {}
        for fn, waits, inc in self.ops:
            for m in waits:
                if seen.get(m.sem.num, 0) < m.value:
                    eng.wait_ge(m.sem, m.value)
                    seen[m.sem.num] = m.value
            ins = fn(eng)
            if inc:
                ins.then_inc(self.sem, 1)


def tt(q, out, a, b, op, *w):
    return q.do(lambda e: e.tensor_tensor(out, a, b, op), *w)


def stt(q, out, a, s, b, op0, op1, *w):
    return q.do(lambda e: e.scalar_tensor_tensor(out, a, s, b, op0, op1), *w)


def ts(q, out, a, s1, s2, op0, op1, *w):
    return q.do(lambda e: e.tensor_scalar(out, a, s1, s2, op0, op1), *w)


def scan(q, out, a, b, init, op0, op1, *w):
    return q.do(lambda e: e.tensor_tensor_scan(out, a, b, init, op0, op1), *w)


def copy(q, out, a, *w):
    return q.do(lambda e: e.tensor_copy(out, a), *w)


def fill(q, out, v, *w):
    return q.do(lambda e: e.memset(out, v), *w)


def act(q, out, a, f, *w, bias=0.0, scale=1.0):
    return q.do(lambda e: e.activation(out, a, f, bias=bias, scale=scale), *w)


def mm(q, out, lhsT, rhs, start, stop, *w, inc=None):
    return q.do(lambda e: e.matmul(out, lhsT, rhs, start=start, stop=stop), *w,
                inc=stop if inc is None else inc)


def rev(ap, backward):
    return ap[:, ::-1] if backward else ap


def program(nc, d):
    with ExitStack() as ctx:
        build(nc, d, ctx)


def build(nc, d, ctx):
    def sb(name, shape, dt=F32):
        return ctx.enter_context(nc.sbuf_tensor(name, shape, dt))

    def sem(name):
        return ctx.enter_context(nc.semaphore(name))

    ident = sb("ident", [128, 128])
    grp = sb("grp", [CP, CP])
    ones = sb("ones", [CP, CP])
    cen = sb("cen", [CP, 2, CP])
    sel = sb("sel", [128, NS, 128], BF16)
    w0 = {m: sb("w0" + m, [CP, CJ, C]) for m in "kvro"}
    vec0 = sb("vec0", [CP, 8, CJ])
    wx = sb("wx", [CP, CJ, 384])
    wz = sb("wz", [CP, CJ, 384])
    vec1 = sb("vec1", [CP, 4, CJ])
    wout = sb("wout", [128, EJ, C])
    bxz = sb("bxz", [128, 3, EJ])
    xpw = [sb(f"xpw{s}", [128, EJ, 128]) for s in range(2)]
    wdt = [sb(f"wdt{s}", [R, 384]) for s in range(2)]
    Am = [sb(f"A{s}", [128, EJ, NS]) for s in range(2)]
    diag = [sb(f"diag{s}", [128, EJ, 4, 128]) for s in range(2)]
    vece = [sb(f"vece{s}", [128, 4, EJ]) for s in range(2)]
    mv = sb("mv", [CP, CJ, 2])
    gs = sb("gs", [CP, 6, CJ])
    st = sb("st", [CP, CJ, NC, 6])
    eps = sb("eps", [128, 1])

    x1 = sb("x1", [CP, CJ, L])
    arena_n = 35848
    arena = sb("arena", [128, arena_n])
    ps = ctx.enter_context(nc.psum_tensor("ps", [128, 8, 512], F32))

    at = [0]

    def take(*shape, parts=128):
        n = 1
        for s in shape:
            n *= s
        o = at[0]
        at[0] += n
        assert at[0] <= arena_n, at[0]
        v = arena[0:parts, o:o + n]
        if len(shape) == 2:
            v = v.rearrange("p (a b) -> p a b", a=shape[0])
        elif len(shape) == 3:
            v = v.rearrange("p (a b c) -> p a b c", a=shape[0], b=shape[1])
        return v

    sems = {}
    for ph in "abc":
        for e in "vaptd":
            sems[ph + e] = sem(f"s_{ph}{e}")
    s_ld = [sem(f"s_ld{i}") for i in range(NC)]
    s_yw = [sem(f"s_yw{i}") for i in range(2)]
    s_yr = [sem(f"s_yr{i}") for i in range(2)]
    s_cw = [sem(f"s_cw{i}") for i in range(2)]
    s_cl = [sem(f"s_cl{i}") for i in range(CG)]
    cd = nc.dram_tensor("c_rows", (2, NS, T), F32, kind="Internal").ap()
    yd = nc.dram_tensor("y_forward", (NC, 128, EJ, T), F32, kind="Internal").ap()

    def x_of(x, b):
        return x[bass.ds(b, 1)].rearrange("o (j p) n -> p (o j) n", p=CP)

    def queues(ph):
        return {e: Queue(sems[ph + e]) for e in "vapt"}

    def ch(c):
        return slice(c * T, (c + 1) * T)

    def stats(V, c):
        for j in range(CJ):
            m = V.do(lambda e, j=j: e.bn_stats(st[:, j, c, :], x1[:, j, ch(c)]), Mark(s_ld[c], 16))
        return m

    q = queues("a")
    V, A, P, PE = q["v"], q["a"], q["p"], q["t"]
    loads = [
        (ident, d["c_ident"]), (grp, d["c_grp"]), (ones, d["c_ones"]), (cen, d["c_cen"]), (sel, d["c_sel"]),
        (w0["k"], d["wk"]), (w0["v"], d["wv"]), (w0["r"], d["wr"]), (w0["o"], d["wo"]),
        (vec0[:, 0:4, :], d["vec0"]), (vec0[:, 7:8, :], d["b_out"]),
        (wx, d["wx"]), (wz, d["wz"]), (vec1, d["vec1"]), (wout, d["wout"]),
    ]
    for s in range(2):
        loads += [(xpw[s], d[f"xpw{s}"]), (wdt[s], d[f"wdt{s}"]), (Am[s], d[f"alog{s}"]),
                  (vece[s][:, 0:3, :], d[f"vece{s}"])]
    tap = take(2, EJ * 4)
    loads += [(tap[:, s, :], d[f"tap{s}"]) for s in range(2)]
    ld = Mark(sems["ad"], 16 * len(loads))

    m = act(A, vec0[:, 4, :], vec0[:, 2, :], ACT.Exp, ld)
    m = ts(V, vec0[:, 4, :], vec0[:, 4, :], -1.0, None, ALU.mult, ALU.bypass, m)
    m = tt(V, vec0[:, 5, :], vec0[:, 4, :], vec0[:, 3, :], ALU.add, ld, m)
    m = ts(V, vec0[:, 5, :], vec0[:, 5, :], 40.0, None, ALU.min, ALU.bypass, m)
    m = act(A, vec0[:, 5, :], vec0[:, 5, :], ACT.Exp, m)
    ts(V, vec0[:, 5, :], vec0[:, 5, :], -1.0, None, ALU.add, ALU.bypass, m)
    for o in range(CJ):
        for j in range(CJ):
            m_bo = mm(PE, ps[0:CP, 0, o:o + 1], w0["o"][:, j, o * CP:(o + 1) * CP],
                      vec0[:, 1, j:j + 1], j == 0, j == 1, ld)
    for i, (w, b) in enumerate(((wx, 1), (wz, 3))):
        for o in range(EJ):
            for j in range(CJ):
                m_bx = mm(PE, ps[:, 1 + i, o:o + 1], w[:, j, o * 128:(o + 1) * 128],
                          vec1[:, b, j:j + 1], j == 0, j == 1)
    copy(V, vec0[:, 6, :], ps[0:CP, 0, 0:CJ], m_bo)
    copy(V, bxz[:, 0, :], ps[:, 1, 0:EJ], m_bx)
    copy(V, bxz[:, 1, :], ps[:, 2, 0:EJ], m_bx)
    ts(V, bxz[:, 2, :], ps[:, 2, 0:EJ], CLAMP, None, ALU.add, ALU.bypass)
    for j in range(CJ):
        ts(V, w0["o"][:, j, :], w0["o"][:, j, :], vec0[:, 0, j:j + 1], None, ALU.mult, ALU.bypass, m_bo)
        ts(V, wx[:, j, :], wx[:, j, :], vec1[:, 0, j:j + 1], None, ALU.mult, ALU.bypass, m_bx)
        ts(V, wz[:, j, :], wz[:, j, :], vec1[:, 2, j:j + 1], None, ALU.mult, ALU.bypass, m_bx)
    fill(V, eps[:, :], 1e-5)
    for s in range(2):
        m = act(A, Am[s][:, :, :], Am[s][:, :, :], ACT.Exp, ld)
        ts(V, Am[s][:, :, :], Am[s][:, :, :], -1.0, None, ALU.mult, ALU.bypass, m)
        ts(V, vece[s][:, 3, :], vece[s][:, 0, :], CLAMP, None, ALU.add, ALU.bypass)
        for j in range(EJ):
            for k in range(4):
                ts(V, diag[s][:, j, k, :], ident[:, :], tap[:, s, 4 * j + k:4 * j + k + 1], None,
                   ALU.mult, ALU.bypass, ld)
    for c in range(1, NC):
        stats(V, c)
    m_setup = [Mark(V.sem, V.count), Mark(A.sem, A.count)]

    with nc.Block() as blk:
        @blk.sync
        def _(e):
            for dst, src in loads:
                e.dma_start(dst[:], src).then_inc(sems["ad"], 16)
            for c in range(NC):
                e.dma_start(x1[:, :, ch(c)], x_of(d["x"], 0)[:, :, ch(c)]).then_inc(s_ld[c], 16)
            for m in m_setup:
                e.wait_ge(m.sem, m.value)

        @blk.scalar
        def _(e):
            A.emit(e)

        @blk.vector
        def _(e):
            V.emit(e)

        @blk.tensor
        def _(e):
            PE.emit(e)

    def group_stats(V, A, PE, banks, after):
        dv, dv2, var = gs[:, 0, :], gs[:, 1, :], gs[:, 2, :]
        pm, pv = (ps[0:CP, b, 0:CJ] for b in banks)
        m1 = mm(PE, pm, grp[:, :], mv[:, :, 0], True, True, *after)
        m = tt(V, dv, mv[:, :, 0], pm, ALU.subtract, m1)
        m = tt(V, dv2, dv, dv, ALU.mult, m)
        m = tt(V, var, mv[:, :, 1], dv2, ALU.add, m)
        m = mm(PE, pv, grp[:, :], var, True, True, m)
        m = ts(V, gs[:, 3, :], pv, 1e-5, None, ALU.add, ALU.bypass, m)
        m = act(A, gs[:, 3, :], gs[:, 3, :], ACT.Ln, m)
        m = act(A, gs[:, 4, :], gs[:, 3, :], ACT.Exp, m, scale=-0.5)
        return stt(V, gs[:, 5, :], pm, -1.0, gs[:, 4, :], ALU.mult, ALU.mult, m)

    def layer0():
        at[0] = 0
        q = queues("b")
        V, A, P, PE = q["v"], q["a"], q["p"], q["t"]
        xn = take(CJ, L, parts=CP)
        kk = take(CJ, L, parts=CP)
        vv = take(CJ, L, parts=CP)
        yy = take(CJ, L, parts=CP)
        Oc = take(3, T + 1, parts=CP)
        s1 = take(3, T, parts=CP)
        s2 = take(4, T, parts=CP)
        bv = take(3, T, parts=CP)
        pp = take(3, T, parts=CP)
        qq = take(3, T, parts=CP)
        rc = take(3, T, parts=CP)
        tn = take(2, T, parts=CP)

        m = stats(V, 0)
        for j in range(CJ):
            m2 = V.do(lambda e, j=j: e.bn_aggr(mv[:, j, :], st[:, j, :, :].rearrange("p a b -> p (a b)")), m)
        m_g = group_stats(V, A, PE, (0, 1), [m2])
        m_xn = {}

        def normalise(c):
            for j in range(CJ):
                m_xn[c] = ts(V, xn[:, j, ch(c)], x1[:, j, ch(c)], gs[:, 4, j:j + 1], gs[:, 5, j:j + 1],
                             ALU.mult, ALU.add, m_g)

        bank_free = {i: m_g for i in range(8)}

        def bank():
            i = next(iter(bank_free))
            return i, [bank_free.pop(i)]

        m_kv = {}
        PROJECT = [("k", kk, 0), ("v", vv, 0), ("k", kk, 1), ("v", vv, 1)]

        def products(c, name, j):
            b, free = bank()
            out = ps[0:CP, b, 0:T]
            for i in range(CJ):
                m = mm(PE, out, w0[name][:, i, j * CP:(j + 1) * CP], xn[:, i, ch(c)],
                       i == 0, i == 1, m_xn[c], *free)
            return b, out, m

        def project(c, outs):
            for name, dst, j in outs:
                b, out, m = products(c, name, j)
                m_kv[name, c, j] = bank_free[b] = act(A, dst[:, j, ch(c)], out, ACT.Copy, m)

        def receptance(c):
            both = [products(c, "r", j) for j in range(CJ)]
            for j, (b, out, _) in enumerate(both):
                o = xn[:, j, ch(c)]
                bank_free[b] = m = act(A, o, out, ACT.Relu, both[1][2], bias=CLAMP)
                m = act(A, o, o, ACT.Exp, m, scale=-1.0, bias=CLAMP)
                m = act(A, o, o, ACT.Ln, m, bias=1.0)
                m_kv["r", c, j] = act(A, o, o, ACT.Exp, m, scale=-1.0)

        units = [(0, c, j) for c in range(NC) for j in range(CJ)]
        units += [(1, c, j) for c in reversed(range(NC)) for j in range(CJ)]
        mO, ms, mB, mP, mN, mI, mD, mT, mY = ({} for _ in range(9))

        def stage1(u):
            s, c, j = units[u]
            r = u % 3
            first = c == (NC - 1 if s else 0)
            edge = T if s else 0
            cur = Oc[:, r, 0:T] if s else Oc[:, r, 1:T + 1]
            prv = Oc[:, r, 1:T + 1] if s else Oc[:, r, 0:T]
            free = [ms[u - 3]] if u >= 3 else []
            if first:
                m = fill(V, Oc[:, r, edge:edge + 1], -1e38, *free)
                init = -1e38
            else:
                ro = (u - 2) % 3
                last = 0 if s else T
                m = copy(V, Oc[:, r, edge:edge + 1], Oc[:, ro, last:last + 1], mO[u - 2], *free)
                init = Oc[:, ro, last:last + 1]
            mO[u] = scan(V, rev(cur, s), vec0[:, 4, j:j + 1].to_broadcast([CP, T]), rev(kk[:, j, ch(c)], s),
                         init, ALU.add, ALU.max, m_kv["k", c, j], m)
            a, b = s1[:, r, :], s2[:, u % 4, :]
            m1 = tt(P, a, prv, cur, ALU.subtract, mO[u], *([mP[u - 3]] if u >= 3 else []))
            m2 = ms[u] = tt(P, b, kk[:, j, ch(c)], cur, ALU.subtract,
                            *([mD[u - 4], mI[u - 4]] if u >= 4 else []))
            act(A, a, a, ACT.Exp, m1, bias=vec0[:, 4, j:j + 1])
            mB[u] = act(A, b, b, ACT.Exp, m2)

        def stage2(u):
            s, c, j = units[u]
            r = u % 3
            a, b = s1[:, r, :], s2[:, u % 4, :]
            first = c == (NC - 1 if s else 0)
            ro, last = (u - 2) % 3, 0 if s else T - 1
            free = [mY[u - 3]] if u >= 3 else []
            m = tt(V, bv[:, r, :], b, vv[:, j, ch(c)], ALU.mult, mB[u], m_kv["v", c, j], *free)
            prev = [mP[u - 2]] if not first else []
            i0 = 0.0 if first else pp[:, ro, last:last + 1]
            i1 = 0.0 if first else qq[:, ro, last:last + 1]
            m1 = scan(V, rev(qq[:, r, :], s), rev(a, s), rev(b, s), i1, ALU.mult, ALU.add, *prev)
            m0 = mP[u] = scan(V, rev(pp[:, r, :], s), rev(a, s), rev(bv[:, r, :], s), i0,
                              ALU.mult, ALU.add, m, *prev)
            m = stt(V, b, b, vec0[:, 5, j:j + 1], qq[:, r, :], ALU.mult, ALU.add, m1)
            mN[u] = stt(V, bv[:, r, :], bv[:, r, :], vec0[:, 5, j:j + 1], pp[:, r, :], ALU.mult, ALU.add, m0)
            m = act(A, rc[:, r, :], b, ACT.Ln, m, *([mT[u - 3]] if u >= 3 else []))
            mI[u] = act(A, rc[:, r, :], rc[:, r, :], ACT.Exp, m, scale=-1.0)

        def stage3(u):
            mD[u] = tt(P, tn[:, u % 2, :], s2[:, u % 4, :], rc[:, u % 3, :], ALU.mult, mI[u],
                       *([mY[u - 2]] if u >= 2 else []))

        m_add = {}

        def stage4(u):
            s, c, j = units[u]
            r = u % 3
            t = tn[:, u % 2, :]
            m = mT[u] = stt(V, t, t, 2.0, rc[:, r, :], ALU.subtract, ALU.mult, mD[u])
            ya = yy[:, j, ch(c)]
            if not s:
                mY[u] = m_add[c, j] = tt(P, ya, bv[:, r, :], t, ALU.mult, m, mN[u])
            else:
                mY[u] = tt(V, t, bv[:, r, :], t, ALU.mult, m, mN[u])

        def stage5(u):
            s, c, j = units[u]
            if s:
                ya = yy[:, j, ch(c)]
                mY[u] = m_add[c, j] = tt(P, ya, ya, tn[:, u % 2, :], ALU.add, mY[u], m_add[c, j])

        def finish(c):
            for j in range(CJ):
                h = yy[:, j, ch(c)]
                m = stt(V, h, h, -0.5, xn[:, j, ch(c)], ALU.mult, ALU.mult, m_add[c, j], m_kv["r", c, j])
            hc = []
            for o in range(CJ):
                b, free = bank()
                for j in range(CJ):
                    m1 = mm(PE, ps[0:CP, b, 0:T], cen[:, int(j != o), :], yy[:, j, ch(c)], j == 0, j == 1, m, *free)
                hc.append((b, ps[0:CP, b, 0:T], m1))
            yield
            for o, (b, h, m1) in enumerate(hc):
                m2 = act(A, xn[:, o, ch(c)], h, ACT.Square, m1)
            yield
            b, free = bank()
            var = ps[0:CP, b, 0:T]
            for j in range(CJ):
                m = mm(PE, var, ones[:, :], xn[:, j, ch(c)], j == 0, j == 1, m2, *free)
            rs = vv[:, 0, ch(c)]
            m = act(A, rs, var, ACT.Ln, m, bias=eps[0:CP, :])
            bank_free[b] = m
            m = act(A, rs, rs, ACT.Exp, m, scale=-0.5)
            yield
            for o, (b, h, _) in enumerate(hc):
                m1 = tt(V, yy[:, o, ch(c)], h, rs, ALU.mult, m)
                bank_free[b] = m1
            yield
            mo = []
            for o in range(CJ):
                b, free = bank()
                for j in range(CJ):
                    m = mm(PE, ps[0:CP, b, 0:T], w0["o"][:, j, o * CP:(o + 1) * CP], yy[:, j, ch(c)],
                           j == 0, j == 1, m1, *free)
                mo.append((b, m))
            yield
            for o, (b, m) in enumerate(mo):
                x = x1[:, o, ch(c)]
                m = bank_free[b] = stt(V, x, ps[0:CP, b, 0:T], vec0[:, 6, o:o + 1], x, ALU.add, ALU.add, m)
                V.do(lambda e, c=c, o=o: e.bn_stats(st[:, o, c, :], x1[:, o, ch(c)]), m)

        n = len(units)
        ends = []

        def advance():
            for g in list(ends):
                if next(g, 0) == 0:
                    ends.remove(g)

        normalise(0)
        project(0, PROJECT)
        normalise(1)
        for u in range(n + 4):
            if u // 2 + 2 < NC and u % 2 == 0:
                normalise(u // 2 + 2)
            if u < n:
                stage1(u)
            if 4 <= u:
                stage4(u - 4)
            if 2 <= u < n + 2:
                stage2(u - 2)
            if u // 2 + 1 < NC:
                project(u // 2 + 1, PROJECT[0:2] if u % 2 == 0 else PROJECT[2:4])
            if n // 2 <= u < n and u % 2 == 0:
                receptance(units[u][1])
            if 3 <= u < n + 3:
                stage3(u - 3)
            if 4 <= u:
                stage5(u - 4)
                advance()
                s, c, j = units[u - 4]
                if s and j == CJ - 1:
                    ends.append(finish(c))
        while ends:
            advance()
        m = Mark(V.sem, V.count)
        for j in range(CJ):
            V.do(lambda e, j=j: e.bn_aggr(mv[:, j, :], st[:, j, :, :].rearrange("p a b -> p (a b)")), m)
        return q

    def layer1():
        at[0] = 0
        q = queues("c")
        V, A, P, PE = q["v"], q["a"], q["p"], q["t"]
        nrm = take(CJ, L, parts=CP)
        yb = [take(EJ, T) for _ in range(2)]
        tmp = take(3, T)
        xh = take(EJ, T + 3)
        mid = xh[:, 0, 0:T // 2].bitcast(BF16)
        xc = [take(EJ, T) for _ in range(2)]
        dt = [take(EJ, T) for _ in range(2)]
        du = [take(EJ, T) for _ in range(2)]
        bcp = [take(T // 2).bitcast(BF16) for _ in range(2)]
        res = take(T)
        NDA, NH, NPR = 6, 6, 8
        cr = take(CG * 4, T)
        da = take(NDA, T)
        hh = take(NH, T)
        pr = take(NPR, T)
        g1, g2 = tmp[:, 0, :], tmp[:, 1, :]
        car = take(NS, EJ)
        ybank, dbank, bbank, wbank = (0, 1, 2), (3, 4), (5, 6), 7

        w_free = {b: [] for b in range(8)}
        w_banks, w_at = [wbank, *ybank, *dbank], [0]

        def w_take():
            b = w_banks[w_at[0] % len(w_banks)]
            w_at[0] += 1
            return b, ps[:, b, 0:T], w_free.pop(b)

        m_g = group_stats(V, A, PE, (5, 6), [])
        m_nrm, m_dt, m_du, m_bcp, m_halo = {}, {}, {}, {}, {}
        last_exp, last_mb, m_back, m_y1 = {}, {}, {}, {}
        chunks = [(0, c) for c in range(NC)] + [(1, c) for c in reversed(range(NC))]

        def norm(c):
            for j in range(CJ):
                m = ts(V, nrm[:, j, ch(c)], x1[:, j, ch(c)], gs[:, 4, j:j + 1], gs[:, 5, j:j + 1],
                       ALU.mult, ALU.add, m_g)
            yield
            b, pw, free = w_take()
            for j in range(CJ):
                if j:
                    yield
                m1 = mm(PE, pw[0:CP, :], ones[:, :], nrm[:, j, ch(c)], j == 0, j == 1, m, *free)
            yield
            for j in range(CJ):
                o = nrm[:, j, ch(c)]
                m = m_hc = tt(V, o, o, pw[0:CP, :], ALU.subtract, m1)
            w_free[b] = [m]
            yield
            for j in range(CJ):
                sq = act(A, tmp[0:CP, j, :], nrm[:, j, ch(c)], ACT.Square, m, *([m_nrm[c - 1]] if c else []))
            yield
            b, pw, free = w_take()
            for j in range(CJ):
                if j:
                    yield
                m = mm(PE, pw[0:CP, :], ones[:, :], tmp[0:CP, j, :], j == 0, j == 1, sq, *free)
            rs = tmp[0:CP, 2, :]
            yield
            m = act(A, rs, pw[0:CP, :], ACT.Ln, m, bias=eps[0:CP, :])
            w_free[b] = [m]
            m = act(A, rs, rs, ACT.Exp, m, scale=-0.5)
            yield
            for j in range(CJ):
                o = nrm[:, j, ch(c)]
                m_nrm[c] = tt(P if c else V, o, o, rs, ALU.mult, m, m_hc)
            yield

        def front(i):
            s, c = chunks[i]
            k2 = i % 2
            if not s:
                yield from norm(c)
            DT, DU, XC, BCP = dt[k2], du[k2], xc[k2], bcp[k2]
            old = [last_exp[i - 2], last_mb[i - 2], *m_back[i - 2]] if i >= 2 else []
            t0 = c * T
            lo, hi = (max(t0 - 3, 0), t0 + T) if not s else (t0, min(t0 + T + 3, L))
            off = lo - (t0 - 3) if not s else 0
            n = hi - lo
            m_pad = []
            prev = [m_halo[i - 1]] if i else []
            if n < T + 3:
                z = xh[:, :, 0:3] if not s else xh[:, :, T:T + 3]
                m_pad = [fill(V, z, 0.0, *prev)]
            mx = {}
            for e in range(EJ):
                b, pw, free = w_take()
                pw = ps[:, b, 0:n]
                for j in range(CJ):
                    if j:
                        yield
                    m = mm(PE, pw, wx[:, j, e * 128:(e + 1) * 128], nrm[:, j, lo:hi],
                           j == 0, j == 1, m_nrm[c], *free)
                yield
                mx[e] = act(A, xh[:, e, off:off + n], pw, ACT.Identity, m, *prev,
                            bias=bxz[:, 0, e:e + 1])
                w_free[b] = [mx[e]]
            m_e, m_z, m_x = {}, {}, {}
            for e in range(EJ + 2):
                if e < EJ:
                    b, pw, free = w_take()
                    for k in range(4):
                        if k:
                            yield
                        o = 3 - k if s else k
                        m = mm(PE, pw, diag[s][:, e, k, :], xh[:, e, o:o + T], k == 0, k == 3,
                               mx[e], *m_pad, *free)
                    m_halo[i] = m
                if 1 <= e <= EJ:
                    m_e[e - 1] = act(A, DT[:, e - 1, :], DT[:, e - 1, :], ACT.Ln, m_e[e - 1], bias=1.0)
                    m_e[e - 1] = act(A, DT[:, e - 1, :], DT[:, e - 1, :], ACT.Exp, m_e[e - 1], scale=-1.0)
                yield
                if e < EJ:
                    m_z[e] = act(A, DU[:, e, :], pw, ACT.Identity, m, *old, bias=vece[s][:, 0, e:e + 1])
                    m = act(A, DT[:, e, :], pw, ACT.Relu, bias=vece[s][:, 3, e:e + 1])
                    w_free[b] = [m]
                    m_e[e] = act(A, DT[:, e, :], DT[:, e, :], ACT.Exp, m, scale=-1.0, bias=CLAMP)
                if e >= 2:
                    m_x[e - 2] = tt(V, XC[:, e - 2, :], DU[:, e - 2, :], DT[:, e - 2, :], ALU.mult,
                                    m_e[e - 2], m_z[e - 2])
                yield
            b, pw, free = w_take()
            for e in range(EJ):
                if e:
                    yield
                m = mm(PE, pw, xpw[s][:, e, :], XC[:, e, :], e == 0, e == EJ - 1, m_x[e], *free)
            yield
            m1 = act(A, BCP[:, :], pw, ACT.Copy, m, *([m_bc_done[i - 2]] if i >= 2 else []))
            m_c = act(A, res[32:64, :], pw[32:64, :], ACT.Copy,
                      *([Mark(s_cw[(i - 1) % 2], 16 * ((i - 1) // 2 + 1))] if i else []))
            m_r = act(A, res[0:R, :], pw[0:R, :], ACT.Copy)
            read = [m_cload[G] for G in range(4 * i - 8, 4 * i - 4)] if i >= 2 else []
            sp.append(([m_c, *read], cd[i % 2], res[48:64, :], s_cw[i % 2]))
            yield
            m = tt(V, res[64:128, :], pw[64:128, :], BCP[64:128, :], ALU.subtract, m1, m_r)
            w_free[b] = [m]
            yield
            act(A, BCP[64:96, :], res[64:96, :], ACT.Copy, m)
            m1 = act(A, mid[96:128, :], res[96:128, :], ACT.Copy, m_halo[i])
            yield
            m_bcp[i] = [m1, tt(V, BCP[96:128, :], res[96:128, :], mid[96:128, :], ALU.subtract, m1)]
            m2, m3, m4 = {}, {}, {}
            for e in range(EJ + 2):
                if e < EJ:
                    b, pw, free = w_take()
                    m = mm(PE, pw, wdt[s][:, e * 128:(e + 1) * 128], res[0:R, :], True, True, m_r, *free)
                if e >= 2:
                    m_dt[i, e - 2] = tt(V, DT[:, e - 2, :], DT[:, e - 2, :], DU[:, e - 2, :], ALU.add,
                                 m4[e - 2], m3[e - 2])
                yield
                if e < EJ:
                    bias = vece[s][:, 1, e:e + 1]
                    m2[e] = act(A, DT[:, e, :], pw, ACT.Abs, m, m_x[e], bias=bias)
                    m3[e] = act(A, DU[:, e, :], pw, ACT.Relu, bias=bias)
                    w_free[b] = [m3[e]]
                    m4[e] = act(A, DT[:, e, :], DT[:, e, :], ACT.Exp, m2[e], scale=-1.0)
                if 1 <= e <= EJ:
                    m4[e - 1] = act(A, DT[:, e - 1, :], DT[:, e - 1, :], ACT.Ln, m4[e - 1], bias=1.0)
                if e >= 2:
                    m_du[i, e - 2] = tt(P if i else V, DU[:, e - 2, :], DT[:, e - 2, :], XC[:, e - 2, :], ALU.mult,
                                        m_dt[i, e - 2])
                yield

        def gate(i):
            s, c = chunks[i]
            last = i == 2 * NC - 1
            mg = {}
            for e in range(EJ):
                b, pw, free = w_take()
                for j in range(CJ):
                    if j:
                        yield
                    m = mm(PE, pw, wz[:, j, e * 128:(e + 1) * 128], nrm[:, j, ch(c)],
                           j == 0, j == 1, *free)
                yield
                free = [mg[e - 1]] if e else ([m_gate[i - 1]] if i - 1 in m_gate else [])
                act(A, g1, pw, ACT.Identity, m, *free, bias=bxz[:, 1, e:e + 1])
                m = act(A, g2, pw, ACT.Relu, bias=bxz[:, 2, e:e + 1])
                w_free[b] = [m]
                m = act(A, g2, g2, ACT.Exp, m, scale=-1.0, bias=CLAMP)
                yield
                m = act(A, g2, g2, ACT.Ln, m, bias=1.0)
                m = act(A, g2, g2, ACT.Exp, m, scale=-1.0)
                yield
                if last:
                    mg[e] = tt(P, xh[:, e, 0:T], g1, g2, ALU.mult, m, m_halo[i], *m_bcp[i])
                else:
                    m = tt(P, g2, g1, g2, ALU.mult, m)
                    yield
                    mg[e] = tt(P, yb[i % 2][:, e, :], yb[i % 2][:, e, :], g2, ALU.mult, m, m_back[i][e])
                yield
            if last:
                while len(m_back.get(i, [])) < EJ:
                    yield
                for e in range(EJ):
                    y = yb[i % 2][:, e, :]
                    mg[e] = tt(V if e == EJ - 1 else P, y, y, xh[:, e, 0:T], ALU.mult, mg[e], m_back[i][e])
            m_gate[i] = mg[EJ - 1]
            for o in range(CJ):
                b, pw, free = w_take()
                pw = pw[0:CP, :]
                for e in range(EJ):
                    if e:
                        yield
                    m = mm(PE, pw, wout[:, e, o * CP:(o + 1) * CP], yb[i % 2][:, e, :],
                           e == 0, e == EJ - 1, mg[e], *free)
                yield
                x = x1[:, o, ch(c)]
                m_gated[i] = m
                m_out[c] = stt(V, x, pw, vec0[:, 7, o:o + 1], x, ALU.add, ALU.add, m)
                w_free[b] = [m_out[c]]
                yield
            if i + 2 < 2 * NC:
                load_y(i + 2)
            sp.append(([m_out[c]], "out", c, sems["cd"]))
            sp.append(([Mark(sems["cd"], 16 * len(m_out))], "next", c, s_ld[c]))

        m_gate, m_out, m_bc_done, m_gated, m_cload, sp = {}, {}, {}, {}, {}, []
        U = [(i, n, e) for i in range(2 * NC) for n in range(NS) for e in range(EJ)]
        N = len(U)
        LC, LT, LM, LB, LA = 1, 4, 1, 3, 4
        m_B, m_exp, m_mb, m_sc, m_mc, m_sum, m_car = ({} for _ in range(7))

        def bcast_b(i, n):
            w = i * NS + n
            prev = [m_mb[w * EJ - 4]] if w >= 2 else []
            m_B[w] = m_bc_done[i] = mm(PE, ps[:, bbank[w % 2], 0:T], sel[:, n, :], bcp[i % 2][:, :], True, True,
                                       *m_bcp[i], *prev)

        def load_c(G):
            i, n = divmod(4 * G, NS)
            k = G % CG
            free = [m_mc[(4 * (G - CG) + 4) * EJ - 1]] if G >= CG else []
            src = cd[i % 2, n:n + 4, :].unsqueeze(0).to_broadcast([128, 4, T])
            sp.append(([Mark(s_cw[i % 2], 16 * (i // 2 + 1)), *free], cr[:, 4 * k:4 * k + 4, :], src, s_cl[k]))
            m_cload[G] = Mark(s_cl[k], 16 * (G // CG + 1))

        def load_y(i):
            c = chunks[i][1]
            w = [Mark(s_yw[b], 16 * sum(1 for k in range(NC) if k % 2 == b)) for b in range(2)]
            if i - 2 >= NC:
                w.append(m_gated[i - 2])
            sp.append((w, yb[i % 2], yd[c], s_yr[i % 2]))

        def mult_b(g):
            i, n, e = U[g]
            w = i * NS + n
            m_mb[g] = tt(V, ps[:, dbank[g % 2], 0:T], du[i % 2][:, e, :], ps[:, bbank[w % 2], 0:T], ALU.mult,
                         m_B[w], m_du[i, e], *([m_sc[g - 2]] if g >= 2 else w_free[dbank[g]]))
            last_mb[i] = m_mb[g]

        def decay(g):
            i, n, e = U[g]
            s = chunks[i][0]
            m_exp[g] = act(A, da[:, g % NDA, :], dt[i % 2][:, e, :], ACT.Exp, m_dt[i, e],
                           *([m_sc[g - NDA]] if g >= NDA else []), scale=Am[s][:, e, n:n + 1])
            last_exp[i] = m_exp[g]

        def step(g):
            i, n, e = U[g]
            s = chunks[i][0]
            init = 0.0 if i % NC == 0 else car[:, n, e:e + 1]
            free = [m_mc[g - NH]] if g >= NH else []
            if g >= NH:
                free.append(m_car[(g - NH) // EJ])
            m_sc[g] = scan(V, rev(hh[:, g % NH, :], s), rev(da[:, g % NDA, :], s),
                           rev(ps[:, dbank[g % 2], 0:T], s), init, ALU.mult, ALU.add,
                           m_exp[g], m_mb[g], *free, *([m_car[(g - NS * EJ) // EJ]] if g >= NS * EJ else []))

        def carry(g):
            i, n, e = U[g]
            s = chunks[i][0]
            last = 0 if s else T - 1
            r = (g - 2) % NH
            m_car[g // EJ] = act(A, car[:, n, :], hh[:, r:r + EJ, last], ACT.Copy, m_sc[g])

        def mult_c(g):
            i, n, e = U[g]
            w = i * NS + n
            m_mc[g] = tt(P, pr[:, g % NPR, :], hh[:, g % NH, :], cr[:, w % (4 * CG), :], ALU.mult,
                         m_sc[g], m_cload[w // 4], *([m_sum[g - NPR]] if g >= NPR else []))

        def total(g):
            i, n, e = U[g]
            free = ([m_y1[i - 1][e]] if i else w_free[ybank[e]]) if n == 0 else []
            m_sum[g] = mm(PE, ps[:, ybank[e], 0:T], ident[:, :], pr[:, g % NPR, :], n == 0, n == NS - 1,
                          m_mc[g], *free, inc=True)
            s, c = chunks[i]
            if s and n == NS - 2:
                o = yb[i % 2][:, e, :]
                m_y1.setdefault(i, {})[e] = stt(V, o, xc[i % 2][:, e, :], vece[s][:, 2, e:e + 1], o, ALU.mult, ALU.add,
                                                Mark(s_yr[i % 2], 16 * ((i - NC) // 2 + 1)))
            if n == NS - 1:
                y = ps[:, ybank[e], 0:T]
                o = yb[i % 2][:, e, :]
                if not s:
                    free = [Mark(s_yw[i % 2], 16 * (i // 2))] if i >= 2 else []
                    m = stt(V, o, xc[i % 2][:, e, :], vece[s][:, 2, e:e + 1], y, ALU.mult, ALU.add, m_sum[g], *free)
                    m_y1.setdefault(i, {})[e] = m
                else:
                    m = tt(V, o, o, y, ALU.add, m_sum[g], m_y1[i][e])
                    m_y1[i][e] = m
                m_back.setdefault(i, []).append(m)
                if e == EJ - 1:
                    if not s:
                        sp.append((m_back[i], yd[i], yb[i % 2], s_yw[i % 2]))
                    if i == NC - 1:
                        load_y(NC)
                        load_y(NC + 1)

        for _ in front(0):
            pass
        w_banks[:] = [wbank]
        NW = 2 * NC * NS
        fronts, gates, waiting, turn = [], [], [], []

        def side():
            for lst in (fronts, gates) if wbank in w_free else turn:
                while lst:
                    turn[:] = [lst]
                    try:
                        next(lst[0])
                        return
                    except StopIteration:
                        lst.pop(0)

        for G in range(CG):
            load_c(G)
        RATE, credit = (1.15, 1.35), 0.0
        for g in range(-5, N + LT):
            w, r = divmod(g + LB, EJ)
            if r == 0 and 0 <= w < NW:
                if w % NS == 0:
                    while fronts:
                        side()
                bcast_b(w // NS, w % NS)
            if 0 <= g < N and g % (NS * EJ) == LT:
                i = g // (NS * EJ)
                if i >= NC + 1:
                    gates.append(gate(i - 1))
                if i + 1 < 2 * NC:
                    fronts.append(front(i + 1))
                else:
                    gates.append(gate(i))
            if 0 <= g < N:
                step(g)
            if 0 <= g + LM < N:
                mult_b(g + LM)
            if 0 <= g + LA < N:
                decay(g + LA)
            if 0 <= g - 1 < N and (g - 1) % EJ == EJ - 1:
                carry(g - 1)
            if 0 <= g - LC < N:
                mult_c(g - LC)
                G = (g - LC) // (4 * EJ)
                if (g - LC) % (4 * EJ) == 4 * EJ - 1 and 4 * (G + CG) < NW:
                    waiting.append(G + CG)
            while waiting and 4 * waiting[0] // NS in m_bcp:
                load_c(waiting.pop(0))
            if 0 <= g - LT < N:
                total(g - LT)
            if g in range(N - 10, N, 2):
                stats(V, NC - 1 - (g - (N - 10)) // 2)
            if 0 <= g < N:
                credit += RATE[chunks[U[g][0]][0]]
            while credit >= 1:
                side()
                credit -= 1
        w_banks[:] = [wbank, *bbank, *dbank]
        for b in bbank:
            w_free[b] = [m_mb[N - 1]]
        for b in dbank:
            w_free[b] = [m_sc[N - 1]]
        while len(gates) > 1:
            side()
        stats(V, 1)
        while gates:
            side()
        return q, sp

    def emit(blk, q):
        @blk.scalar
        def _(e):
            e.preload_act_table_set("natural_log_exp_and_others")
            q["a"].emit(e)

        @blk.vector
        def _(e):
            q["v"].emit(e)

        @blk.tensor
        def _(e):
            q["t"].emit(e)

    q0 = layer0()
    q1, sp1 = layer1()
    nb = [sems["b" + e].num for e in "vapt"] + [s.num for s in s_ld]
    ncl = [sems["c" + e].num for e in "vaptd"] + [s.num for s in s_yw + s_yr + s_cw + s_cl]

    def clear(e, nums):
        for k in nums:
            e.sem_clear(range(k, k + 1))

    with nc.Fori(0, B) as b:
        xnext, xout = x_of(d["x"][1:B + 1], b), x_of(d["out"], b)
        with nc.Block() as blk:
            @blk.gpsimd
            def _(e):
                clear(e, ncl)
                q0["p"].emit(e)

            emit(blk, q0)
        with nc.Block() as blk:
            @blk.sync
            def _(e):
                for waits, dst, src, done in sp1:
                    for m in waits:
                        e.wait_ge(m.sem, m.value)
                    if dst == "out":
                        dst, src = xout[:, :, ch(src)], x1[:, :, ch(src)]
                    elif dst == "next":
                        dst, src = x1[:, :, ch(src)], xnext[:, :, ch(src)]
                    e.dma_start(dst, src).then_inc(done, 16)
                e.wait_ge(sems["cd"], 16 * NC)

            @blk.gpsimd
            def _(e):
                clear(e, nb)
                q1["p"].emit(e)

            emit(blk, q1)

    with nc.Block() as blk:
        @blk.sync
        def _(e):
            for k in s_ld:
                e.wait_ge(k, 16)


def kernel(**inputs):
    import ml_dtypes
    import numpy as np
    import concourse.bacc as bacc
    from concourse.bass_utils import run_bass_kernel_spmd

    v = {k: np.asarray(a) for k, a in inputs.items()}
    l0, l1 = "L0_conv_", "L1_conv_"

    def wt(a, p):
        t = a.T
        return np.ascontiguousarray(t.reshape(t.shape[0] // p, p, t.shape[1]).transpose(1, 0, 2))

    def cols(names, p):
        return np.ascontiguousarray(np.stack([v[n].reshape(-1, p).T for n in names], axis=1))

    arrays = {
        "x": np.concatenate([v["x"].reshape(B, C, L), np.zeros((1, C, L), v["x"].dtype)]),
        "c_ident": np.eye(128, dtype=np.float32),
        "c_grp": np.kron(np.eye(CP // 6), np.ones((6, 6)) / 6).astype(np.float32),
        "c_ones": np.full((CP, CP), 1.0 / C, np.float32),
        "c_cen": np.stack([np.eye(CP) - 1.0 / C, np.full((CP, CP), -1.0 / C)], axis=1).astype(np.float32),
        "wk": wt(v[l0 + "Wk"], CP), "wv": wt(v[l0 + "Wv"], CP),
        "wr": wt(v[l0 + "Wr"], CP), "wo": wt(v[l0 + "Wo"], CP),
        "vec0": cols([l0 + "ln_g", l0 + "ln_b", l0 + "w_decay", l0 + "u"], CP),
        "b_out": cols([l1 + "b_out"], CP),
        "wx": wt(v[l1 + "W_in_x"], CP), "wz": wt(v[l1 + "W_in_z"], CP),
        "vec1": cols([l1 + "g1", l1 + "b1", l1 + "g2", l1 + "b2"], CP),
        "wout": wt(v[l1 + "W_out"], 128),
    }
    sel = np.zeros((128, NS, 128), np.float32)
    for part in range(1, 4):
        for n in range(NS):
            sel[32 * part + n, n, :] = 1
    arrays["c_sel"] = sel.astype(ml_dtypes.bfloat16)
    for s, sfx in enumerate("fb"):
        w = wt(v[l1 + "W_xproj_" + sfx], 128)
        xp = np.zeros((128, EJ, 128), np.float32)
        xp[:, :, 0:R] = w[:, :, 0:R]
        for part in range(1, 4):
            xp[:, :, 32 * part:32 * part + 2 * NS] = w[:, :, R:]
        arrays[f"xpw{s}"] = xp
        arrays[f"wdt{s}"] = np.ascontiguousarray(v[l1 + "W_dt_" + sfx].T)
        arrays[f"alog{s}"] = np.ascontiguousarray(
            v[l1 + "A_log_" + sfx].reshape(EJ, 128, NS).transpose(1, 0, 2))
        arrays[f"vece{s}"] = cols([l1 + "conv_b_" + sfx, l1 + "dt_bias_" + sfx, l1 + "D_" + sfx], 128)
        arrays[f"tap{s}"] = np.ascontiguousarray(
            v[l1 + "conv_w_" + sfx].reshape(EJ, 128, 4).transpose(1, 0, 2).reshape(128, EJ * 4))

    nc = bacc.Bacc("TRN2", target_bir_lowering=False, num_devices=1)
    d = {k: nc.dram_tensor("in_" + k, a.shape, mybir.dt.from_np(a.dtype), kind="ExternalInput").ap()
         for k, a in arrays.items()}
    d["out"] = nc.dram_tensor("out_0", (B, C, L), F32, kind="ExternalOutput").ap()
    program(nc, d)
    r = run_bass_kernel_spmd(nc, [{"in_" + k: a for k, a in arrays.items()}], core_ids=[0])
    return r.results[0]["out_0"].reshape(B, C, 56, 56)
```
